# Optimizing a Trainium2 kernel written in Bass

```python
import numpy as np
import jax
import jax.numpy as jnp

def _softmax(x, axis=-1):
    return jax.nn.softmax(x, axis=axis)

def _gelu(x):
    return jax.nn.gelu(x, approximate=True)

def _silu(x):
    return jax.nn.silu(x)

def _sigmoid(x):
    return jax.nn.sigmoid(x)

def _layernorm(x, axis=-1, eps=1e-05):
    m = jnp.mean(x, axis=axis, keepdims=True)
    v = jnp.var(x, axis=axis, keepdims=True)
    return (x - m) / jnp.sqrt(v + eps)

def _scatter_add(tgt, idx, src, axis=0):
    return tgt.at[idx].add(src)

def _segment_sum(src, seg, n):
    return jax.ops.segment_sum(src, seg, n)
kernel_name = 'mk_flamingo_gated_d4_seqx_r8_309f21'

def setup_inputs(seed: int=0):
    np.random.seed(seed)
    _w = jnp.asarray

    def _rec_inputs():
        import jax
        import jax.numpy as jnp
        _rk = jax.random.key(seed)
        x = 7.22e-05 + 1 * jax.random.normal(jax.random.fold_in(_rk, 1), (2, 512, 128), jnp.float32)
        _lenS = 512 - jax.random.randint(jax.random.fold_in(_rk, 7), (2,), 0, max(1, 512 // 4) + 1, jnp.int32)
        _lenS2 = 77 - jax.random.randint(jax.random.fold_in(_rk, 8), (2,), 0, max(1, 77 // 4) + 1, jnp.int32)
        _ctx_1024P = jax.random.normal(jax.random.fold_in(_rk, 11), (2, 16, 128), jnp.float32)
        _ctx_1024c = jax.random.dirichlet(jax.random.fold_in(_rk, 511), 0.3 * jnp.ones((16,), jnp.float32), (2, 77))
        _ctx_1024t = jnp.einsum('bsk,bkd->bsd', _ctx_1024c, _ctx_1024P)
        _ctx_1024t = _ctx_1024t * jax.lax.rsqrt(jnp.mean(jnp.square(_ctx_1024t)) + 1e-12) * 0.953939
        ctx_1024 = -0.000514642 + 1.00011 * (_ctx_1024t + 0.3 * jax.random.normal(jax.random.fold_in(_rk, 611), (2, 77, 128), jnp.float32))
        _validS = jnp.arange(512)[None, :] < _lenS[:, None]
        _validS2 = jnp.arange(77)[None, :] < _lenS2[:, None]
        _causal = jnp.tril(jnp.ones((512, 512), dtype=bool))
        mask_Bx1xSxS2_if1 = jnp.where(jnp.ones((2, 1, 512, 77), dtype=bool), 1, 0).astype(jnp.int32)
        _g = jax.random.normal(jax.random.fold_in(_rk, 9001), (2, 4), jnp.float32)
        _g = jnp.sign(_g) * jnp.maximum(jnp.abs(_g), 1.0) + (_g == 0) * 1.0
        g_xattn = _g[0]
        g_ffn = _g[1]
        return (x, ctx_1024, mask_Bx1xSxS2_if1, g_xattn, g_ffn)
    x, ctx_1024, mask_Bx1xSxS2_if1, g_xattn, g_ffn = _rec_inputs()

    def _L0_xattn_setup():
        import jax, jax.numpy as jnp
        import numpy as np
        B, L_ENC, L_DEC, D = (16, 64, 128, 128)
        key = jax.random.key(seed)
        k1, k2, k3, k4, k5, k6 = jax.random.split(key, 6)
        encoder_hc = jax.random.normal(k1, (B, L_ENC, D), dtype=jnp.float32)
        decoder_hq = jax.random.normal(k2, (B, L_DEC, D), dtype=jnp.float32)
        w_sim = jax.random.normal(k3, (3 * D,), dtype=jnp.float32) * 0.02
        b_sim = jax.random.normal(k4, (1,), dtype=jnp.float32) * 0.02
        W_qv = jax.random.normal(k5, (4 * D, D), dtype=jnp.float32) * 0.02
        b_qv = jax.random.normal(k6, (D,), dtype=jnp.float32) * 0.02
        return {'encoder_hc': encoder_hc, 'decoder_hq': decoder_hq, 'w_sim': w_sim, 'b_sim': b_sim, 'W_qv': W_qv, 'b_qv': b_qv}
    _L0_xattn_all = _L0_xattn_setup()
    _L0_xattn_in = {k: v for k, v in _L0_xattn_all.items() if k in ('w_sim', 'b_sim', 'W_qv', 'b_qv')}
    del _L0_xattn_all

    def _L0_ffn_setup():
        import jax, jax.numpy as jnp
        import numpy as np
        H = 128
        I = 4 * H
        E = 8
        TOP_K = 2
        key = jax.random.key(seed)
        ks = jax.random.split(key, 6)
        s = 0.02
        hidden_states = jax.random.normal(ks[0], (4, 512, H), dtype=jnp.float32)
        w1_shared = jax.random.normal(ks[1], (H, I), dtype=jnp.float32) * s
        w2_shared = jax.random.normal(ks[2], (I, H), dtype=jnp.float32) * s
        w1_routed = jax.random.normal(ks[3], (E, H, I), dtype=jnp.float32) * s
        w2_routed = jax.random.normal(ks[4], (E, I, H), dtype=jnp.float32) * s
        w_router = jax.random.normal(ks[5], (H, E), dtype=jnp.float32) * s
        return {'hidden_states': hidden_states, 'w1_shared': w1_shared, 'w2_shared': w2_shared, 'w1_routed': w1_routed, 'w2_routed': w2_routed, 'w_router': w_router}
    _L0_ffn_all = _L0_ffn_setup()
    _L0_ffn_in = {k: v for k, v in _L0_ffn_all.items() if k in ('w1_shared', 'w2_shared', 'w1_routed', 'w2_routed', 'w_router')}
    del _L0_ffn_all

    def _L1_xattn_setup():
        import jax, jax.numpy as jnp
        import numpy as np
        DIM = 128
        H = 16
        DH = 64
        INNER = H * DH
        SCALE = DH ** (-0.5)
        key = jax.random.key(seed)
        ks = jax.random.split(key, 6)
        B, L, R = (4, 512, 64)
        x = jax.random.normal(ks[0], (B, L, DIM), dtype=jnp.float32)
        context = jax.random.normal(ks[1], (B, R, DIM), dtype=jnp.float32)
        s = DIM ** (-0.5)
        Wq = jax.random.normal(ks[2], (DIM, INNER), dtype=jnp.float32) * s
        Wk = jax.random.normal(ks[3], (DIM, INNER), dtype=jnp.float32) * s
        Wv = jax.random.normal(ks[4], (DIM, INNER), dtype=jnp.float32) * s
        Wo = jax.random.normal(ks[5], (INNER, DIM), dtype=jnp.float32) * INNER ** (-0.5)
        return {'x': x, 'context': context, 'Wq': Wq, 'Wk': Wk, 'Wv': Wv, 'Wo': Wo}
    _L1_xattn_all = _L1_xattn_setup()
    _L1_xattn_in = {k: v for k, v in _L1_xattn_all.items() if k in ('Wq', 'Wk', 'Wv', 'Wo')}
    del _L1_xattn_all

    def _L1_ffn_setup():
        import jax, jax.numpy as jnp
        import numpy as np
        QP = 127.0
        MIN_RANGE = 1e-06

        def _ste_round(x):
            return x + jax.lax.stop_gradient(jnp.round(x) - x)

        def _quant_per_tensor(x):
            scale = jnp.maximum(jnp.max(jnp.abs(x)), MIN_RANGE) / QP
            return (_ste_round(x / scale), scale)

        def _qlinear(x2d, w, b):
            xq, sx = _quant_per_tensor(x2d)
            wq, sw = _quant_per_tensor(w)
            out = jnp.matmul(xq, wq.T) + b[None, :]
            return out * (sw * sx)
        key = jax.random.key(seed)
        k = jax.random.split(key, 5)
        B, N, D, H = (8, 128, 128, 512)
        return {'x': jax.random.normal(k[0], (B, N, D), dtype=jnp.float32), 'w1': jax.random.normal(k[1], (H, D), dtype=jnp.float32) * 0.02, 'b1': jax.random.normal(k[2], (H,), dtype=jnp.float32) * 0.02, 'w2': jax.random.normal(k[3], (D, H), dtype=jnp.float32) * 0.02, 'b2': jax.random.normal(k[4], (D,), dtype=jnp.float32) * 0.02}
    _L1_ffn_all = _L1_ffn_setup()
    _L1_ffn_in = {k: v for k, v in _L1_ffn_all.items() if k in ('w1', 'b1', 'w2', 'b2')}
    del _L1_ffn_all

    def _L2_xattn_setup():
        import jax, jax.numpy as jnp
        import numpy as np
        from math import sqrt
        H = 16
        key = jax.random.key(seed)
        ks = jax.random.split(key, 8)
        B, Sq, Skv, Dq, Dkv, Dall = (2, 256, 256, 128, 128, 128)
        x = jax.random.normal(ks[0], (B, Sq, Dq), dtype=jnp.float32)
        y = jax.random.normal(ks[1], (B, Skv, Dkv), dtype=jnp.float32)
        attention_mask = jnp.ones((B, 1, Sq, Skv), dtype=jnp.int32)
        Wq = jax.random.normal(ks[2], (Dall, Dq), dtype=jnp.float32) * 0.02
        Wk = jax.random.normal(ks[3], (Dall, Dkv), dtype=jnp.float32) * 0.02
        Wv = jax.random.normal(ks[4], (Dall, Dkv), dtype=jnp.float32) * 0.02
        Wo = jax.random.normal(ks[5], (Dq, Dall), dtype=jnp.float32) * 0.02
        bo = jnp.zeros((Dq,), dtype=jnp.float32)
        return {'x': x, 'y': y, 'attention_mask': attention_mask, 'Wq': Wq, 'Wk': Wk, 'Wv': Wv, 'Wo': Wo, 'bo': bo}
    _L2_xattn_all = _L2_xattn_setup()
    _L2_xattn_in = {k: v for k, v in _L2_xattn_all.items() if k in ('Wq', 'Wk', 'Wv', 'Wo', 'bo')}
    del _L2_xattn_all

    def _L2_ffn_setup():
        import jax, jax.numpy as jnp
        import numpy as np
        HIDDEN = 128
        INNER = 512

        def _weight_quant(w):
            scale = 1.0 / jnp.clip(jnp.mean(jnp.abs(w)), 1e-05)
            wq = jnp.clip(jnp.round(w * scale), -1.0, 1.0) / scale
            return w + jax.lax.stop_gradient(wq - w)

        def _act_quant(x):
            scale = 127.0 / jnp.clip(jnp.max(jnp.abs(x), axis=-1, keepdims=True), 1e-05)
            xq = jnp.clip(jnp.round(x * scale), -128.0, 127.0) / scale
            return x + jax.lax.stop_gradient(xq - x)

        def _bitlinear(x, w):
            return jnp.einsum('bsi,oi->bso', _act_quant(x), _weight_quant(w))
        key = jax.random.key(seed)
        k0, k1, k2, k3 = jax.random.split(key, 4)
        x = jax.random.normal(k0, (4, 256, HIDDEN), dtype=jnp.float32)
        w_gate = jax.random.normal(k1, (INNER, HIDDEN), dtype=jnp.float32) / np.sqrt(HIDDEN)
        w_up = jax.random.normal(k2, (INNER, HIDDEN), dtype=jnp.float32) / np.sqrt(HIDDEN)
        w_down = jax.random.normal(k3, (HIDDEN, INNER), dtype=jnp.float32) / np.sqrt(INNER)
        return {'x': x, 'w_gate': w_gate, 'w_up': w_up, 'w_down': w_down}
    _L2_ffn_all = _L2_ffn_setup()
    _L2_ffn_in = {k: v for k, v in _L2_ffn_all.items() if k in ('w_gate', 'w_up', 'w_down')}
    del _L2_ffn_all

    def _L3_xattn_setup():
        import jax, jax.numpy as jnp
        import numpy as np
        EMBED_DIM = 128
        B, LQ, LK = (4, 256, 256)
        key = jax.random.key(seed)
        ks = jax.random.split(key, 9)
        d = EMBED_DIM
        s = 1.0 / np.sqrt(d)
        return {'query': jax.random.normal(ks[0], (B, LQ, d), dtype=jnp.float32), 'key': jax.random.normal(ks[1], (B, LK, d), dtype=jnp.float32), 'value': jax.random.normal(ks[2], (B, LK, d), dtype=jnp.float32), 'Wq': jax.random.uniform(ks[3], (d, d), jnp.float32, -s, s), 'bq': jax.random.uniform(ks[4], (d,), jnp.float32, -s, s), 'Wk': jax.random.uniform(ks[5], (d, d), jnp.float32, -s, s), 'bk': jax.random.uniform(ks[6], (d,), jnp.float32, -s, s), 'Wv': jax.random.uniform(ks[7], (d, d), jnp.float32, -s, s), 'bv': jax.random.uniform(ks[8], (d,), jnp.float32, -s, s)}
    _L3_xattn_all = _L3_xattn_setup()
    _L3_xattn_in = {k: v for k, v in _L3_xattn_all.items() if k in ('Wq', 'bq', 'Wk', 'bk', 'Wv', 'bv')}
    del _L3_xattn_all

    def _L3_ffn_setup():
        import jax, jax.numpy as jnp
        import numpy as np
        D_MODEL = 128
        D_FF = 512
        NUM_EXPERTS = 8
        B, N = (16, 128)
        key = jax.random.key(seed)
        ks = jax.random.split(key, 7)
        s_in = 1.0 / np.sqrt(D_MODEL)
        s_ff = 1.0 / np.sqrt(D_FF)
        return {'x': jax.random.normal(ks[0], (B, N, D_MODEL), dtype=jnp.float32), 'Wr': jax.random.uniform(ks[1], (D_MODEL, NUM_EXPERTS), jnp.float32, -s_in, s_in), 'br': jax.random.uniform(ks[2], (NUM_EXPERTS,), jnp.float32, -s_in, s_in), 'W1': jax.random.uniform(ks[3], (NUM_EXPERTS, D_MODEL, D_FF), jnp.float32, -s_in, s_in), 'b1': jax.random.uniform(ks[4], (NUM_EXPERTS, D_FF), jnp.float32, -s_in, s_in), 'W2': jax.random.uniform(ks[5], (NUM_EXPERTS, D_FF, D_MODEL), jnp.float32, -s_ff, s_ff), 'b2': jax.random.uniform(ks[6], (NUM_EXPERTS, D_MODEL), jnp.float32, -s_ff, s_ff)}
    _L3_ffn_all = _L3_ffn_setup()
    _L3_ffn_in = {k: v for k, v in _L3_ffn_all.items() if k in ('Wr', 'br', 'W1', 'b1', 'W2', 'b2')}
    del _L3_ffn_all
    return {'x': x, 'ctx_1024': ctx_1024, 'mask_Bx1xSxS2_if1': mask_Bx1xSxS2_if1, 'g_xattn': g_xattn, 'g_ffn': g_ffn, 'L0_xattn_w_sim': _L0_xattn_in['w_sim'], 'L0_xattn_b_sim': _L0_xattn_in['b_sim'], 'L0_xattn_W_qv': _L0_xattn_in['W_qv'], 'L0_xattn_b_qv': _L0_xattn_in['b_qv'], 'L0_ffn_w1_shared': _L0_ffn_in['w1_shared'], 'L0_ffn_w2_shared': _L0_ffn_in['w2_shared'], 'L0_ffn_w1_routed': _L0_ffn_in['w1_routed'], 'L0_ffn_w2_routed': _L0_ffn_in['w2_routed'], 'L0_ffn_w_router': _L0_ffn_in['w_router'], 'L1_xattn_Wq': _L1_xattn_in['Wq'], 'L1_xattn_Wk': _L1_xattn_in['Wk'], 'L1_xattn_Wv': _L1_xattn_in['Wv'], 'L1_xattn_Wo': _L1_xattn_in['Wo'], 'L1_ffn_w1': _L1_ffn_in['w1'], 'L1_ffn_b1': _L1_ffn_in['b1'], 'L1_ffn_w2': _L1_ffn_in['w2'], 'L1_ffn_b2': _L1_ffn_in['b2'], 'L2_xattn_Wq': _L2_xattn_in['Wq'], 'L2_xattn_Wk': _L2_xattn_in['Wk'], 'L2_xattn_Wv': _L2_xattn_in['Wv'], 'L2_xattn_Wo': _L2_xattn_in['Wo'], 'L2_xattn_bo': _L2_xattn_in['bo'], 'L2_ffn_w_gate': _L2_ffn_in['w_gate'], 'L2_ffn_w_up': _L2_ffn_in['w_up'], 'L2_ffn_w_down': _L2_ffn_in['w_down'], 'L3_xattn_Wq': _L3_xattn_in['Wq'], 'L3_xattn_bq': _L3_xattn_in['bq'], 'L3_xattn_Wk': _L3_xattn_in['Wk'], 'L3_xattn_bk': _L3_xattn_in['bk'], 'L3_xattn_Wv': _L3_xattn_in['Wv'], 'L3_xattn_bv': _L3_xattn_in['bv'], 'L3_ffn_Wr': _L3_ffn_in['Wr'], 'L3_ffn_br': _L3_ffn_in['br'], 'L3_ffn_W1': _L3_ffn_in['W1'], 'L3_ffn_b1': _L3_ffn_in['b1'], 'L3_ffn_W2': _L3_ffn_in['W2'], 'L3_ffn_b2': _L3_ffn_in['b2']}

def reference(x, ctx_1024, mask_Bx1xSxS2_if1, g_xattn, g_ffn, L0_xattn_w_sim, L0_xattn_b_sim, L0_xattn_W_qv, L0_xattn_b_qv, L0_ffn_w1_shared, L0_ffn_w2_shared, L0_ffn_w1_routed, L0_ffn_w2_routed, L0_ffn_w_router, L1_xattn_Wq, L1_xattn_Wk, L1_xattn_Wv, L1_xattn_Wo, L1_ffn_w1, L1_ffn_b1, L1_ffn_w2, L1_ffn_b2, L2_xattn_Wq, L2_xattn_Wk, L2_xattn_Wv, L2_xattn_Wo, L2_xattn_bo, L2_ffn_w_gate, L2_ffn_w_up, L2_ffn_w_down, L3_xattn_Wq, L3_xattn_bq, L3_xattn_Wk, L3_xattn_bk, L3_xattn_Wv, L3_xattn_bv, L3_ffn_Wr, L3_ffn_br, L3_ffn_W1, L3_ffn_b1, L3_ffn_W2, L3_ffn_b2):
    import jax
    import jax.numpy as jnp

    def _L0_xattn_ref(encoder_hc, decoder_hq, w_sim, b_sim, W_qv, b_qv):
        import jax, jax.numpy as jnp
        import numpy as np
        B, L_ENC, L_DEC, D = (16, 64, 128, 128)
        d = encoder_hc.shape[-1]
        w1, w2, w3 = (w_sim[:d], w_sim[d:2 * d], w_sim[2 * d:])
        Sim = (encoder_hc @ w1)[:, :, None] + (decoder_hq @ w2)[:, None, :] + jnp.einsum('bid,bjd->bij', encoder_hc * w3, decoder_hq) + b_sim[0]
        A = jax.nn.softmax(Sim, axis=2)
        hq_hat = jnp.einsum('bij,bjd->bid', A, decoder_hq)
        Batt = jax.nn.softmax(jnp.max(Sim, axis=2), axis=1)
        hc_bar = jnp.einsum('bi,bid->bd', Batt, encoder_hc)[:, None, :]
        hc_hat = jnp.broadcast_to(hc_bar, encoder_hc.shape)
        feats = jnp.concatenate([encoder_hc, hq_hat, encoder_hc * hq_hat, encoder_hc * hc_hat], axis=-1)
        hcq = feats @ W_qv + b_qv
        return hcq

    def _L0_ffn_ref(hidden_states, w1_shared, w2_shared, w1_routed, w2_routed, w_router):
        import jax, jax.numpy as jnp
        import numpy as np
        H = 128
        I = 4 * H
        E = 8
        TOP_K = 2
        bsz, seq_len, hidden_dim = hidden_states.shape
        flat = hidden_states.reshape(-1, hidden_dim)
        shared_out = jax.nn.silu(flat @ w1_shared) @ w2_shared
        router_logits = flat @ w_router
        routing_weights = jax.nn.softmax(router_logits, axis=-1)
        topk_w, topk_idx = jax.lax.top_k(routing_weights, TOP_K)
        topk_w = topk_w / jnp.sum(topk_w, axis=-1, keepdims=True)
        one_hot = jax.nn.one_hot(topk_idx, E, dtype=topk_w.dtype)
        cw = jnp.einsum('tk,tke->te', topk_w, one_hot)
        routed_out = jnp.zeros_like(flat)
        for e in range(E):
            expert_out = jax.nn.silu(flat @ w1_routed[e]) @ w2_routed[e]
            routed_out = routed_out + cw[:, e:e + 1] * expert_out
        total = shared_out + routed_out
        return total.reshape(bsz, seq_len, hidden_dim)

    def _L1_xattn_ref(x, context, Wq, Wk, Wv, Wo):
        import jax, jax.numpy as jnp
        import numpy as np
        DIM = 128
        H = 16
        DH = 64
        INNER = H * DH
        SCALE = DH ** (-0.5)
        B, L, _ = x.shape
        R = context.shape[1]
        q = (x @ Wq).reshape(B, L, H, DH).transpose(0, 2, 1, 3)
        k = (context @ Wk).reshape(B, R, H, DH).transpose(0, 2, 1, 3)
        v = (context @ Wv).reshape(B, R, H, DH).transpose(0, 2, 1, 3)
        scores = jnp.einsum('bhld,bhrd->bhlr', q, k) * SCALE
        attn = jax.nn.softmax(scores, axis=-1)
        out = jnp.einsum('bhlr,bhrd->bhld', attn, v)
        out = out.transpose(0, 2, 1, 3).reshape(B, L, INNER)
        return out @ Wo

    def _L1_ffn_ref(x, w1, b1, w2, b2):
        import jax, jax.numpy as jnp
        import numpy as np
        QP = 127.0
        MIN_RANGE = 1e-06

        def _ste_round(x):
            return x + jax.lax.stop_gradient(jnp.round(x) - x)

        def _quant_per_tensor(x):
            scale = jnp.maximum(jnp.max(jnp.abs(x)), MIN_RANGE) / QP
            return (_ste_round(x / scale), scale)

        def _qlinear(x2d, w, b):
            xq, sx = _quant_per_tensor(x2d)
            wq, sw = _quant_per_tensor(w)
            out = jnp.matmul(xq, wq.T) + b[None, :]
            return out * (sw * sx)
        B, N, D = x.shape
        h = _qlinear(x.reshape(-1, D), w1, b1)
        h = jax.nn.gelu(h, approximate=False)
        o = _qlinear(h, w2, b2)
        return o.reshape(B, N, -1)

    def _L2_xattn_ref(x, y, attention_mask, Wq, Wk, Wv, Wo, bo):
        import jax, jax.numpy as jnp
        import numpy as np
        from math import sqrt
        H = 16
        B, Sq, _ = x.shape
        Dall = Wq.shape[0]
        Dh = Dall // H
        q = (x @ Wq.T).reshape(B, Sq, H, Dh).transpose(0, 2, 1, 3)
        k = (y @ Wk.T).reshape(B, -1, H, Dh).transpose(0, 2, 1, 3)
        v = (y @ Wv.T).reshape(B, -1, H, Dh).transpose(0, 2, 1, 3)
        scores = jnp.einsum('bhqd,bhkd->bhqk', q, k)
        mask = attention_mask == 0
        scores = jnp.where(mask, jnp.float32(-1000000000.0), scores)
        attn = jax.nn.softmax(scores / sqrt(Dh), axis=-1)
        out = jnp.einsum('bhqk,bhkd->bhqd', attn, v)
        out = out.transpose(0, 2, 1, 3).reshape(B, Sq, Dall)
        return out @ Wo.T + bo

    def _L2_ffn_ref(x, w_gate, w_up, w_down):
        import jax, jax.numpy as jnp
        import numpy as np
        HIDDEN = 128
        INNER = 512

        def _weight_quant(w):
            scale = 1.0 / jnp.clip(jnp.mean(jnp.abs(w)), 1e-05)
            wq = jnp.clip(jnp.round(w * scale), -1.0, 1.0) / scale
            return w + jax.lax.stop_gradient(wq - w)

        def _act_quant(x):
            scale = 127.0 / jnp.clip(jnp.max(jnp.abs(x), axis=-1, keepdims=True), 1e-05)
            xq = jnp.clip(jnp.round(x * scale), -128.0, 127.0) / scale
            return x + jax.lax.stop_gradient(xq - x)

        def _bitlinear(x, w):
            return jnp.einsum('bsi,oi->bso', _act_quant(x), _weight_quant(w))
        gate = jax.nn.silu(_bitlinear(x, w_gate))
        up = _bitlinear(x, w_up)
        return _bitlinear(gate * up, w_down)

    def _L3_xattn_ref(query, key, value, Wq, bq, Wk, bk, Wv, bv):
        import jax, jax.numpy as jnp
        import numpy as np
        EMBED_DIM = 128
        B, LQ, LK = (4, 256, 256)
        scale = jnp.asarray(EMBED_DIM ** 0.5, query.dtype)
        Q = jnp.einsum('bqd,ed->bqe', query, Wq) + bq
        K = jnp.einsum('bkd,ed->bke', key, Wk) + bk
        V = jnp.einsum('bkd,ed->bke', value, Wv) + bv
        scores = jnp.einsum('bqe,bke->bqk', Q, K) / scale
        weights = jax.nn.softmax(scores, axis=-1)
        return jnp.einsum('bqk,bke->bqe', weights, V)

    def _L3_ffn_ref(x, Wr, br, W1, b1, W2, b2):
        import jax, jax.numpy as jnp
        import numpy as np
        D_MODEL = 128
        D_FF = 512
        NUM_EXPERTS = 8
        B, N = (16, 128)
        scores = jnp.einsum('bh,he->be', x.mean(axis=1), Wr) + br
        top1 = jnp.argmax(scores, axis=-1)
        w1 = W1[top1]
        c1 = b1[top1]
        w2 = W2[top1]
        c2 = b2[top1]
        h = jax.nn.relu(jnp.einsum('bnh,bhf->bnf', x, w1) + c1[:, None, :])
        out = jnp.einsum('bnf,bfh->bnh', h, w2) + c2[:, None, :]
        return out
    x = x + jnp.tanh(g_xattn[0]) * _L0_xattn_ref(_layernorm(x, axis=-1), ctx_1024, L0_xattn_w_sim, L0_xattn_b_sim, L0_xattn_W_qv, L0_xattn_b_qv)
    x = x + jnp.tanh(g_ffn[0]) * _L0_ffn_ref(_layernorm(x, axis=-1), L0_ffn_w1_shared, L0_ffn_w2_shared, L0_ffn_w1_routed, L0_ffn_w2_routed, L0_ffn_w_router)
    x = x + jnp.tanh(g_xattn[1]) * _L1_xattn_ref(_layernorm(x, axis=-1), ctx_1024, L1_xattn_Wq, L1_xattn_Wk, L1_xattn_Wv, L1_xattn_Wo)
    x = x + jnp.tanh(g_ffn[1]) * _L1_ffn_ref(_layernorm(x, axis=-1), L1_ffn_w1, L1_ffn_b1, L1_ffn_w2, L1_ffn_b2)
    x = x + jnp.tanh(g_xattn[2]) * _L2_xattn_ref(_layernorm(x, axis=-1), ctx_1024, mask_Bx1xSxS2_if1, L2_xattn_Wq, L2_xattn_Wk, L2_xattn_Wv, L2_xattn_Wo, L2_xattn_bo)
    x = x + jnp.tanh(g_ffn[2]) * _L2_ffn_ref(_layernorm(x, axis=-1), L2_ffn_w_gate, L2_ffn_w_up, L2_ffn_w_down)
    x = x + jnp.tanh(g_xattn[3]) * _L3_xattn_ref(_layernorm(x, axis=-1), ctx_1024, ctx_1024, L3_xattn_Wq, L3_xattn_bq, L3_xattn_Wk, L3_xattn_bk, L3_xattn_Wv, L3_xattn_bv)
    x = x + jnp.tanh(g_ffn[3]) * _L3_ffn_ref(_layernorm(x, axis=-1), L3_ffn_Wr, L3_ffn_br, L3_ffn_W1, L3_ffn_b1, L3_ffn_W2, L3_ffn_b2)
    return x

_drawn_inputs = setup_inputs


def setup_inputs(seed=0):
    import zlib

    import numpy as np

    out = dict(_drawn_inputs(seed))
    spreads = {'L2_xattn_bo': (0.0, 0.1)}
    factors = {'g_ffn': 7.241,
     'L0_xattn_w_sim': 3.182,
     'L0_xattn_b_qv': 3.475,
     'L1_ffn_b1': 64.0,
     'L1_ffn_b2': 64.0,
     'L2_xattn_Wq': 8.0,
     'L2_xattn_Wk': 8.0,
     'L2_xattn_Wv': 3.26,
     'L2_xattn_Wo': 3.385,
     'L3_xattn_bq': 29.784,
     'L3_xattn_bk': 64.0,
     'L3_ffn_b1': 3.776,
     'L3_ffn_b2': 3.021}
    for name, (base, spread) in spreads.items():
        noise = np.random.default_rng([zlib.crc32(name.encode()), seed]).standard_normal(out[name].shape)
        drawn = base * np.exp(spread * noise) if base else spread * noise
        out[name] = jnp.asarray(drawn.astype(out[name].dtype))
    for name, factor in factors.items():
        out[name] = (out[name] * factor).astype(out[name].dtype)
    return out
```

```python
from contextlib import ExitStack

import numpy as np
import concourse.bass as bass
from concourse import mybir

ALU = mybir.AluOpType
ACT = mybir.ActivationFunctionType
F32 = mybir.dt.float32
BF16 = mybir.dt.bfloat16
I32 = mybir.dt.int32
U32 = mybir.dt.uint32
AX = mybir.AxisListType.X
RMAX = bass.bass_isa.ReduceOp.max
RADD = bass.bass_isa.ReduceOp.add

P = 128
B, SEQ, D = 2, 512, 128
TB = SEQ // P
T = B * TB
R = 77
E = 8
FF = 512
C = FF // P
H = 16
HR = H * R
CH = -(-HR // P)
HB = 512 // R
HEADS = [(h, min(h + HB, H)) for h in range(0, H, HB)]
DH1, DH2 = 64, D // H
NK1 = H * DH1 // P
HALVES = [(h0, h1) for half in (0, H // 2) for h0, h1 in ((half, half + HB), (half + HB, half + H // 2))]
TCH = [(c, min(c + 4, CH)) for c in range(0, CH, 4)]
EPS = 1e-5
MAGIC = 1.5 * 2.0 ** 23
MASKED = -(2.0 ** 100)
GUESS = 1593268703.0
QP = 127.0
LAYERS = ["L0x", "L0f", "L1x", "L1f", "L2x", "L2f", "L3x", "L3f"]


class Ring:

    def __init__(self, banks, full, free, keys):
        self.banks, self.full_sems, self.free_sems = banks, full, free
        self.use = {k: (i % len(banks), i // len(banks)) for i, k in enumerate(keys)}
        assert len(self.use) == len(keys)

    def bank(self, key):
        return self.banks[self.use[key][0]]

    def full(self, key):
        return self.full_sems[self.use[key][0]]

    def free(self, key):
        return self.free_sems[self.use[key][0]]

    def reused(self, key):
        return self.use[key][1] > 0

    def freed_before(self, key):
        return self.free(key), self.use[key][1]

    def filled(self, key):
        return self.full(key), self.use[key][1] + 1

    def freed(self, key):
        return self.free(key), self.use[key][1] + 1


def bank_keys():
    s = ["cb0"]
    s += [("kv1", w, i) for w in range(2) for i in range(3)]
    s += [("m1", b, i) for b in range(B) for i in range(len(HALVES))]
    s += [("n1T", b, i) for b in range(B) for i in range(len(HALVES))]
    s += ["kv2", "k3", "m3", "v3"]
    t = [("n1", b, i) for b in range(B) for i in range(len(TCH))]
    t += [("v2", b, i) for b in range(B) for i in range(len(TCH))]
    o = []
    t += [("lnT", "L0x", b) for b in range(B)]
    s += [("sim", b) for b in range(B)]
    s += [("hc", b) for b in range(B)]
    t += [("aT0", b) for b in range(B)]
    s += [("hq", b) for b in range(B)]
    o += [("L0x", b) for b in range(B)]
    t += [("lnT", "L0f", b) for b in range(B)]
    s += [("router", b) for b in range(B)]
    for b in range(B):
        for e in range(E + 1):
            s += [("h0", b, e, c) for c in range(C)]
            o.append(("y0", b, e))
    for layer in ("L1x", "L2x"):
        t += [("lnT", layer, b) for b in range(B)]
        if layer == "L2x":
            s += [("q2", b) for b in range(B)]
        s += [(layer, 0, i) for i in range(len(HEADS))]
        for n in range(T):
            if n + 1 < T:
                s += [(layer, n + 1, i) for i in range(len(HEADS))]
            t += [("pT", layer, n, i) for i in range(len(TCH))]
            if n % TB == 0:
                o.append((layer, n // TB))
            if n % TB == TB - 1 and layer == "L2x":
                o.append(("o2", n // TB))
        if layer == "L1x":
            t += [("xqT", "L1f", b) for b in range(B)]
            s += [("h1", b, c) for b in range(B) for c in range(C)]
            o += [("L1f", b) for b in range(B)]
    t += [("xqT", "L2f", b) for b in range(B)]
    s += [(w, n) for n in range(T) for w in ("gate", "up")]
    t += [("guT", n) for n in range(T)]
    o += [("L2f", b) for b in range(B)]
    t += [("lnT", "L3x", b) for b in range(B)]
    s += [("s3", b) for b in range(B)]
    t += [("aT3", b) for b in range(B)]
    o += [("L3x", b) for b in range(B)]
    t += [("lnT", "L3f", b) for b in range(B)]
    s += [("mean", b) for b in range(B)]
    s += [("pick", b) for b in range(B)]
    s += [("h3", b, c) for b in range(B) for c in range(C)]
    o += [("L3f", b) for b in range(B)]
    return s, t, o


def program(nc, a, out):
    ctx = ExitStack()
    with ctx:
        def sb(name, shape, dt=F32):
            return ctx.enter_context(nc.sbuf_tensor(name, shape, dt))

        def sem(name):
            return ctx.enter_context(nc.semaphore(name))

        x = sb("x", [P, T, D])
        ctx_rows = sb("ctx_rows", [R, B, D])
        ctxT = sb("ctxT", [P, B, R])
        gates = sb("gates", [P, 8])
        simw = sb("simw", [P, 3])
        b_sim = sb("b_sim", [1, 1])
        wqv0 = sb("wqv0", [P, 4, D])
        row_bqv0 = sb("row_bqv0", [1, D])
        row_bo2 = sb("row_bo2", [1, D])
        row_bv3 = sb("row_bv3", [1, D])
        w_router = sb("w_router", [P, E])
        experts = sb("experts", [P, E + 1, 2, FF])
        wqT1 = sb("wqT1", [P, H * DH1 // P, D])
        wkv1 = sb("wkv1", [P, 2, H * DH1])
        wo1 = sb("wo1", [P, H * DH1 // P, D])
        fw1 = sb("fw1", [P, FF])
        fb1 = sb("fb1", [P, C])
        fw2 = sb("fw2", [P, C, D])
        b2_1 = sb("b2_1", [P, D])
        w2x = sb("w2x", [P, 4, D])
        fw_gu = sb("fw_gu", [P, 2, FF])
        fw_d = sb("fw_d", [P, C, D])
        w3x = sb("w3x", [P, 3, D])
        b3x = sb("b3x", [P, 2])
        wr3 = sb("wr3", [P, E])
        br3 = sb("br3", [1, E])
        b1_3 = sb("b1_3", [P, E, C])

        ident = sb("ident", [P, P])
        identb = sb("identb", [P, P], BF16)
        ones = sb("ones", [P, P])
        iota8 = sb("iota8", [P, E])
        headmask = sb("headmask", [P, H])
        inv_seq = sb("inv_seq", [P, 1])
        G = sb("G", [P, 8])

        m0 = sb("m0", [P, B, R])
        cb0 = sb("cb0_row", [1, B * R])
        m1 = sb("m1", [P, B, HR])
        n1 = sb("n1", [P, B, CH, D])
        nT = sb("nT", [P, HR])
        kv2T = sb("kv2T", [P, 2, B * R])
        k2blk = sb("k2blk", [P, B, H, R])
        v2 = sb("v2", [P, B, CH, D])
        k3T = sb("k3T", [P, B * R])
        m3 = sb("m3", [P, B * R])
        cb3 = sb("cb3_row", [1, B * R])
        v3 = sb("v3", [R, B, D])
        penalty = sb("penalty", [P, T, R], BF16)
        fw1q = sb("fw1q", [P, FF], BF16)
        fw2q = sb("fw2q", [P, C, D], BF16)
        guq = sb("guq", [P, 2, FF], BF16)
        dq = sb("dq", [P, C, D], BF16)
        wstat = sb("wstat", [P, 8])
        wall = sb("wall", [P, 8])
        wsc = sb("wsc", [P, 20])

        bn = sb("bn", [P, T, 6])
        mv = sb("mv", [P, T, 2])
        rstd = sb("rstd", [P, T])
        newton = sb("newton", [P, B, 3, TB])
        ln = sb("ln", [P, T, D])
        lnT = sb("lnT", [P, T, P])
        lnTf = lnT[:, :, :].rearrange("p t n -> p (t n)")
        att = sb("att", [P, B, TB, R])
        attT = sb("attT", [R, B, TB * P])
        amax = sb("amax", [P, B, TB])
        asum = sb("asum", [P, B, TB])
        hqT = sb("hqT", [P, B, TB * P])
        prodT = sb("prodT", [P, B, TB * P])
        bat = sb("bat", [P, B, 12])
        wb0 = sb("wb0", [P, B, D])
        logits = sb("logits", [P, B, TB, E])
        top = sb("top", [P, B, TB, 8])
        topi = sb("topi", [P, B, TB, 8], U32)
        topf = sb("topf", [P, B, TB, 8])
        tw = sb("tw", [P, B, 4, TB])
        cw = sb("cw", [P, B, TB, E])
        cw2 = sb("cw2", [P, B, TB, E])
        hT = sb("hT", [P, 2, C, TB * P])
        acc = sb("acc", [P, B, TB, D])
        pr = sb("pr", [P, 2, HR])
        prT = sb("prT", [P, 2, CH, P])
        pmax = sb("pmax", [P, 2, H])
        psums = sb("psums", [P, 2, 2, H])
        xqb = sb("xqb", [P, T, D], BF16)
        xqT = sb("xqT", [P, T * P], BF16)
        hmax = sb("hmax", [P, B * C + 2])
        hall = sb("hall", [P, 2])
        tsc = sb("tsc", [P, 8, T])
        gub = sb("gub", [P, 2, FF], BF16)
        mean3 = sb("mean3", [P, B])
        sc3 = sb("sc3", [1, B, 8])
        top3 = sb("top3", [1, B, 8])
        top3i = sb("top3i", [1, B, 8], U32)
        b1s = sb("b1s", [P, B, C])
        kv1T = hT[:, :, :, :].rearrange("p n c k -> p (n c k)")[:, 0:2 * NK1 * B * R].rearrange(
            "p (w c r) -> p w c r", w=2, c=NK1)
        silu = pr[:, :, 0:FF]
        guf = prT[:, :, 0:C, :].rearrange("p n c k -> p n (c k)")
        hqb = wkv1[:, :, :].rearrange("p w n -> p (w n)").bitcast(BF16).rearrange("p (c n) -> p c n", c=C)
        guT = hqb[:, :, :].rearrange("p c n -> p (c n)").rearrange("p (t c k) -> p t c k", t=T, c=C)
        qtmp = wqT1[:, :, :].rearrange("p (b t) d -> p b t d", b=B)
        b2s = wb0[0:1, :, :]
        mask = att[:, :, :, :].rearrange("p b t r -> p (b t) r").bitcast(I32)
        q2T = hqT
        o2T = hqT
        w1s = prodT
        w2s = acc[:, :, :, :].rearrange("p b t d -> p b (t d)")
        ctxTf = ctxT[:, :, :].rearrange("p b r -> p (b r)")
        ex_flat = experts[:, :, :, :].rearrange("p e w n -> p (e w n)")
        b1_flat = b1_3[:, :, :].rearrange("p e c -> p (e c)")
        b2_flat = nT[0:1, 0:E * D]

        def flat(w):
            return w[:, :, :].rearrange("p c k -> p (c k)")


        banks = [ctx.enter_context(nc.psum_tensor(f"bank{i}", [P, 512], F32)) for i in range(8)]
        s_keys, t_keys, o_keys = bank_keys()

        def ring(name, part, keys):
            return Ring(part, [sem(f"{name}{i}_full") for i in range(len(part))],
                        [sem(f"{name}{i}_free") for i in range(len(part))], keys)

        S = ring("S", banks[0:4], s_keys)
        TR = ring("T", banks[4:6], t_keys)
        O = ring("O", banks[6:8], o_keys)

        DMAS = {"x0": 1, "x1": 1, "ctx": 4, "gates": 2, "l0x": 3, "l1x": 4, "l2x": 2, "l3x": 3, "mask": 1,
                "l1f": 4, "l2f": 2, "l3f": 6, **{f"expert{k}": 2 for k in range(E + 1)}}
        ld_sem = {n: sem("loaded_" + n) for n in DMAS}

        def loaded(name):
            return ld_sem[name], 16 * DMAS[name]

        const_ready = sem("const_ready")
        pool_step = sem("pool_step")
        dve_step = sem("dve_step")
        gates_ready = sem("gates_ready")
        m0_ready = sem("m0_ready")
        v2T_ready = sem("v2T_ready")
        pen_ready = sem("pen_ready")
        wstat_ready = sem("wstat_ready")
        wall_ready = sem("wall_ready")
        wq_ready = sem("wq_ready")
        ln_ready = sem("ln_ready")
        xq_ready = sem("xq_ready")
        att_exp = sem("att_exp")
        att_ready = sem("att_ready")
        bmax_ready = sem("bmax_ready")
        bmax_all = sem("bmax_all")
        bat_sub = sem("bat_sub")
        bat_exp = sem("bat_exp")
        prod_ready = sem("prod_ready")
        wb0_ready = sem("wb0_ready")
        gap_ready = sem("gap_ready")
        gap_exp = sem("gap_exp")
        p_exp = sem("p_exp")
        p_recip = sem("p_recip")
        p_ready = sem("p_ready")
        pT_used = sem("pT_used")
        amax_ready = sem("amax_ready")
        amax_all = sem("amax_all")
        s1_ready = sem("s1_ready")
        hq_ready = sem("hq_ready")
        tscale_ready = sem("tscale_ready")
        silu_ready = sem("silu_ready")
        gub_ready = sem("gub_ready")
        pick_ready = sem("pick_ready")
        x_final = sem("x_final")
        stored = sem("stored")

        def ln_done(layer, b):
            return ln_ready, 2 * LAYERS.index(layer) + b + 1

        def lnT_done(layer, b):
            return TR.freed(("lnT", layer, b))

        def pT_read(layer, n):
            if n % TB == TB - 1:
                return O.filled((layer, n // TB))
            g = T * (layer == "L2x") + n
            return pT_used, g + 1 - g // TB

        block = ctx.enter_context(nc.Block())

        @block.sync
        def _(sp):
            def ld(name, dst, src):
                sp.dma_start(dst, src).then_inc(ld_sem[name], 16)

            xr = a["x"].rearrange("b (t p) d -> p (b t) d", p=P)
            ld("x0", x[:, 0:TB, :], xr[:, 0:TB, :])
            ld("ctx", ctxT[:, :, :], a["ctxT"])
            ld("ctx", simw[:, :], a["simw"])
            ld("x1", x[:, TB:T, :], xr[:, TB:T, :])
            ld("mask", mask[:, :, :], a["mask"].rearrange("b (t p) r -> p (b t) r", p=P))
            ld("ctx", ctx_rows[:, :, :], a["ctx_rows"])
            ld("ctx", b_sim[:, :], a["b_sim"])
            ld("l1x", wkv1[:, 0, :], a["wk1"])
            ld("l1x", wkv1[:, 1, :], a["wv1"])
            ld("l1x", wqT1[:, :, :], a["wqT1"])
            ld("l1x", wo1[:, :, :], a["wo1"])
            ld("l0x", wqv0[:, :, :], a["wqv0"])
            ld("l0x", row_bqv0[:, :], a["bqv0"])
            ld("l0x", w_router[:, :], a["w_router"])
            ld("l2x", w2x[:, :, :], a["w2x"])
            ld("l2x", row_bo2[:, :], a["bo2"])
            ld("l3x", w3x[:, :, :], a["w3x"])
            ld("l3x", b3x[:, :], a["b3x"])
            ld("l3x", row_bv3[:, :], a["bv3"])
            for k in range(E + 1):
                ld(f"expert{k}", experts[:, k, 0, :], a["w1_0"][:, k, :])
                ld(f"expert{k}", experts[:, k, 1, :], a["w2_0"][:, k, :])
            ld("l1f", fw1[:, :], a["fw1"])
            ld("l1f", fw2[:, :, :], a["fw2"])
            ld("l1f", fb1[:, :], a["fb1"])
            ld("l1f", b2_1[:, :], a["b2_1"].partition_broadcast(P))
            ld("l2f", fw_gu[:, :, :], a["fw_gu"])
            ld("l2f", fw_d[:, :, :], a["fw_d"])
            ld("l3f", wr3[:, :], a["wr3"])
            ld("l3f", br3[:, :], a["br3"])
            ld("l3f", b1_3[:, :, :], a["b1_3"])
            sp.wait_ge(*O.filled(("y0", B - 1, E)))
            ld("l3f", b2_flat, a["b2_3"])
            ld("l3f", experts[:, 0:E, 0, :], a["w1_3"])
            ld("l3f", experts[:, 0:E, 1, :], a["w2_3"])
            outr = out.rearrange("b (t p) d -> p (b t) d", p=P)
            for b in range(B):
                sp.wait_ge(x_final, b + 1)
                sp.dma_start(outr[:, b * TB:b * TB + TB, :], x[:, b * TB:b * TB + TB, :]).then_inc(stored, 16)
            sp.wait_ge(stored, 16 * B)

        @block.gpsimd
        def _(pool):
            pool.dma_start(gates[:, 0:4], a["g_xattn"].partition_broadcast(P)).then_inc(ld_sem["gates"], 16)
            pool.dma_start(gates[:, 4:8], a["g_ffn"].partition_broadcast(P)).then_inc(ld_sem["gates"], 16)
            pool.memset(ident[:, :], 0.0).then_inc(pool_step, 1)
            pool.memset(headmask[:, :], 1.0).then_inc(pool_step, 1)
            pool.memset(ones[:, :], 1.0)
            pool.memset(inv_seq[:, :], 1.0 / SEQ)
            pool.iota(iota8[:, :], pattern=[[1, E]], base=0, channel_multiplier=0,
                      allow_small_or_imprecise_dtypes=True).then_inc(const_ready, 1)
            pool.wait_ge(pool_step, 2)
            pool.affine_select(out=ident[:, :], in_=ident[:, :], compare_op=ALU.not_equal, fill=1.0,
                               base=0, pattern=[[-1, P]], channel_multiplier=1).then_inc(const_ready, 1)
            pool.affine_select(out=headmask[:, :], in_=headmask[:, :], compare_op=ALU.is_ge, fill=0.0,
                               base=0, pattern=[[-DH2, H]], channel_multiplier=1).then_inc(pool_step, 1)
            pool.wait_ge(pool_step, 3)
            pool.affine_select(out=headmask[:, :], in_=headmask[:, :], compare_op=ALU.is_ge, fill=0.0,
                               base=DH2 - 1, pattern=[[DH2, H]], channel_multiplier=-1).then_inc(const_ready, 1)
            pool.wait_ge(const_ready, 2)
            pool.tensor_copy(identb[:, :], ident[:, :]).then_inc(const_ready, 1)
            for b in range(B):
                pool.wait_ge(bmax_ready, b + 1)
                pool.partition_all_reduce(bat[:, b, 1:2], bat[:, b, 0:1], P, RMAX).then_inc(bmax_all, 1)
            pool.wait_ge(wstat_ready, 1)
            pool.partition_all_reduce(wall[:, 0:2], wstat[:, 0:2], P, RMAX)
            pool.partition_all_reduce(wall[:, 2:5], wstat[:, 2:5], P, RADD).then_inc(wall_ready, 1)

            def normalise(layer):
                for n in range(T):
                    pool.wait_ge(p_recip, T * (layer == "L2x") + n + 1)
                    v = pr[:, n % 2, :].rearrange("p (h r) -> p h r", h=H)
                    pool.tensor_tensor(v, v, psums[:, n % 2, 1, :].unsqueeze(2).to_broadcast([P, H, R]),
                                       ALU.mult).then_inc(p_ready, 1)

            normalise("L1x")
            for i in range(2):
                pool.wait_ge(amax_ready, i + 1)
                pool.partition_all_reduce(hall[:, i:i + 1], hmax[:, B * C + i:B * C + i + 1], P,
                                          RMAX).then_inc(amax_all, 1)
            normalise("L2x")

        @block.scalar
        def _(act):
            def copy_out(ring_, key, dst, src):
                act.wait_ge(*ring_.filled(key))
                act.activation(dst, src, ACT.Copy).then_inc(ring_.free(key), 1)

            def copy_chunks(key, dst, c0, c1):
                bank = TR.bank(key)
                act.wait_ge(*TR.filled(key))
                full = min(c1, HR // P)
                ins = act.activation(dst[:, c0:full, :],
                                     bank[:, 0:(full - c0) * P].rearrange("p (c k) -> p c k", k=P), ACT.Copy)
                if full < c1:
                    ins = act.activation(dst[0:HR - full * P, full, :],
                                         bank[0:HR - full * P, (full - c0) * P:(full - c0 + 1) * P], ACT.Copy)
                ins.then_inc(TR.free(key), 1)

            def transposed(layer, b):
                copy_out(TR, ("lnT", layer, b), lnTf[:, b * SEQ:b * SEQ + SEQ], TR.bank(("lnT", layer, b))[:, :])

            def quantised(layer, b):
                copy_out(TR, ("xqT", layer, b), xqT[:, b * SEQ:b * SEQ + SEQ],
                         TR.bank(("xqT", layer, b))[:, :].bitcast(BF16)[:, 0:SEQ])

            act.wait_ge(*loaded("gates"))
            act.activation(G[:, :], gates[:, :], ACT.Tanh).then_inc(gates_ready, 1)
            for w in range(2):
                for i in range(3):
                    n = min(3, NK1 - 3 * i)
                    copy_out(S, ("kv1", w, i), kv1T[:, w, 3 * i:3 * i + n, :],
                             S.bank(("kv1", w, i))[:, 0:n * B * R].rearrange("p (c r) -> p c r", c=n))
            for b in range(B):
                for i, (h0, h1) in enumerate(HALVES):
                    copy_out(S, ("m1", b, i), m1[:, b, h0 * R:h1 * R], S.bank(("m1", b, i))[:, 0:(h1 - h0) * R])
            for b in range(B):
                if b:
                    act.wait_ge(*TR.filled(("n1", b - 1, len(TCH) - 1)))
                for i, (h0, h1) in enumerate(HALVES):
                    copy_out(S, ("n1T", b, i), nT[:, h0 * R:h1 * R], S.bank(("n1T", b, i))[:, 0:(h1 - h0) * R])
                for i, (c0, c1) in enumerate(TCH):
                    copy_chunks(("n1", b, i), n1[:, b, :, :], c0, c1)
            copy_out(S, "kv2", kv2T[:, :, :], S.bank("kv2")[:, 0:2 * B * R].rearrange("p (w r) -> p w r", w=2))
            act.wait_ge(*loaded("l3x"))
            act.wait_ge(*S.filled("k3"))
            act.activation(k3T[:, :], S.bank("k3")[:, 0:B * R], ACT.Identity, bias=b3x[:, 1:2]).then_inc(S.free("k3"), 1)
            act.wait_ge(*S.filled("m3"))
            act.activation(cb3[:, :], S.bank("m3")[0:1, B * R:2 * B * R], ACT.Copy)
            act.activation(m3[:, :], S.bank("m3")[:, 0:B * R], ACT.Copy).then_inc(S.free("m3"), 1)
            copy_out(S, "v3", v3[:, :, :], S.bank("v3")[0:R, 0:B * D].rearrange("r (b d) -> r b d", b=B))
            for b in range(B):
                for i, (c0, c1) in enumerate(TCH):
                    copy_chunks(("v2", b, i), v2[:, b, :, :], c0, c1)

            for b in range(B):
                transposed("L0x", b)
            for b in range(B):
                act.wait_ge(*S.freed(("sim", b)))
                act.activation(att[:, b, :, :], att[:, b, :, :], ACT.Exp).then_inc(att_exp, 1)
                act.wait_ge(bat_sub, b + 1)
                act.activation(bat[:, b, 8:12], bat[:, b, 8:12], ACT.Exp,
                               accum_out=bat[:, b, 2:3]).then_inc(bat_exp, 1)
            for b in range(B):
                copy_out(TR, ("aT0", b), attT[:, b, :], TR.bank(("aT0", b))[0:R, :])
            for b in range(B):
                copy_out(S, ("hq", b), hqT[:, b, :], S.bank(("hq", b))[:, :])

            for b in range(B):
                transposed("L0f", b)
            for b in range(B):
                act.wait_ge(gap_ready, b + 1)
                act.activation(tw[:, b, 1, :], tw[:, b, 0, :], ACT.Exp).then_inc(gap_exp, 1)
            for b in range(B):
                for k in range(E + 1):
                    n = b * (E + 1) + k
                    for c in range(C):
                        key = ("h0", b, k, c)
                        act.wait_ge(*S.filled(key))
                        if n >= 2 and c == 0:
                            act.wait_ge(*O.filled(("y0", (n - 2) // (E + 1), (n - 2) % (E + 1))))
                        act.activation(hT[:, n % 2, c, :], S.bank(key)[:, :], ACT.Silu).then_inc(S.free(key), 1)
                    if b == B - 1 and k == 4:
                        transposed("L1x", 0)

            def attention(layer, scale):
                base = T * (layer == "L2x")

                def exps(n):
                    act.wait_ge(*S.freed((layer, n, len(HEADS) - 1)))
                    act.activation(pr[:, n % 2, :], pr[:, n % 2, :], ACT.Exp, scale=scale).then_inc(p_exp, 1)

                if layer == "L2x":
                    for b in range(B):
                        copy_out(S, ("q2", b), q2T[:, b, :], S.bank(("q2", b))[:, :])
                exps(0)
                for n in range(T):
                    if n + 1 < T:
                        exps(n + 1)
                    if n >= 2:
                        act.wait_ge(*pT_read(layer, n - 2))
                    for i, (c0, c1) in enumerate(TCH):
                        copy_chunks(("pT", layer, n, i), prT[:, n % 2, :, :], c0, c1)
                    if layer == "L2x" and n == TB:
                        copy_out(O, ("L2x", 0), o2T[:, 0, :], O.bank(("L2x", 0))[:, :])
                if layer == "L2x":
                    copy_out(O, ("L2x", 1), o2T[:, 1, :], O.bank(("L2x", 1))[:, :])

            transposed("L1x", 1)
            attention("L1x", DH1 ** -0.5)
            for b in range(B):
                quantised("L1f", b)
            act.wait_ge(s1_ready, 1)
            for b in range(B):
                for c in range(C):
                    key = ("h1", b, c)
                    act.wait_ge(*S.filled(key))
                    act.activation(hT[:, b, c, :], S.bank(key)[:, :], ACT.Gelu, bias=wsc[:, 4 + c:5 + c],
                                   scale=wsc[:, 2:3]).then_inc(S.free(key), 1)
            for b in range(B):
                transposed("L2x", b)
            attention("L2x", DH2 ** -0.5)
            for b in range(B):
                quantised("L2f", b)
            for n in range(T + 1):
                if n < T:
                    act.wait_ge(tscale_ready, n // TB + 1)
                    if n >= 2:
                        act.wait_ge(*S.freed(("up", n - 2)))
                    act.wait_ge(*S.filled(("gate", n)))
                    act.activation(silu[:, n % 2, :], S.bank(("gate", n))[:, :], ACT.Silu,
                                   scale=tsc[:, 2, n:n + 1]).then_inc(S.free(("gate", n)), 1)
                if n >= 1:
                    m = n - 1
                    copy_out(TR, ("guT", m), guT[:, m, :, :],
                             TR.bank(("guT", m))[:, :].bitcast(BF16)[:, 0:FF].rearrange("p (c k) -> p c k", c=C))
            for b in range(B):
                transposed("L3x", b)
            for b in range(B):
                act.wait_ge(*S.freed(("s3", b)))
                act.activation(att[:, b, :, :], att[:, b, :, :], ACT.Exp, scale=D ** -0.5).then_inc(att_exp, 1)
            for b in range(B):
                copy_out(TR, ("aT3", b), attT[:, b, :], TR.bank(("aT3", b))[0:R, :])
            for b in range(B):
                transposed("L3f", b)
            for b in range(B):
                act.wait_ge(pick_ready, b + 1)
                for c in range(C):
                    key = ("h3", b, c)
                    act.wait_ge(*S.filled(key))
                    act.activation(hT[:, b, c, :], S.bank(key)[:, :], ACT.Relu,
                                   bias=b1s[:, b, c:c + 1]).then_inc(S.free(key), 1)

        @block.tensor
        def _(pe):
            def acquire(ring_, key):
                if ring_.reused(key):
                    pe.wait_ge(*ring_.freed_before(key))
                return ring_.bank(key)

            def transpose_rows(layer, b):
                key = ("lnT", layer, b)
                bank = acquire(TR, key)
                pe.wait_ge(*ln_done(layer, b))
                for t in range(TB):
                    ins = pe.transpose(bank[:, t * P:t * P + P], ln[:, b * TB + t, :], ident[:, :])
                ins.then_inc(TR.full(key), 1)

            def transpose_quantised(layer, b):
                key = ("xqT", layer, b)
                bank = acquire(TR, key)[:, :].bitcast(BF16)
                pe.wait_ge(xq_ready, B * (layer == "L2f") + b + 1)
                for t in range(TB):
                    ins = pe.transpose(bank[:, t * P:t * P + P], xqb[:, b * TB + t, :], identb[:, :])
                ins.then_inc(TR.full(key), 1)

            def transpose_chunks(key, src, c0, c1, id_):
                bank = acquire(TR, key)
                for c in range(c0, c1):
                    n = min(P, HR - c * P)
                    ins = pe.transpose(bank[0:n, (c - c0) * P:(c - c0 + 1) * P], src[:, c * P:c * P + n], id_[:, :])
                ins.then_inc(TR.full(key), 1)

            pe.wait_ge(*loaded("ctx"))
            bank = acquire(S, "cb0")
            pe.matmul(bank[0:1, 0:B * R], simw[:, 1:2], ctxTf, start=True, stop=True).then_inc(S.full("cb0"), 1)
            pe.wait_ge(*loaded("l1x"))
            for w in range(2):
                for i in range(3):
                    bank = acquire(S, ("kv1", w, i))
                    for c in range(3 * i, min(3 * i + 3, NK1)):
                        ins = pe.matmul(bank[:, (c - 3 * i) * B * R:(c - 3 * i + 1) * B * R],
                                        wkv1[:, w, c * P:c * P + P], ctxTf, start=True, stop=True)
                    ins.then_inc(S.full(("kv1", w, i)), 1)

            def per_head(name, b, w, weight):
                for i, (h0, h1) in enumerate(HALVES):
                    key = (name, b, i)
                    bank = acquire(S, key)
                    pe.wait_ge(*S.freed(("kv1", w, 2)))
                    for h in range(h0, h1):
                        p0, c = DH1 * (h // NK1), h % NK1
                        ins = pe.matmul(bank[:, (h - h0) * R:(h - h0 + 1) * R], weight[p0:p0 + DH1, c, :],
                                        kv1T[p0:p0 + DH1, w, c, b * R:b * R + R], start=True, stop=True)
                    ins.then_inc(S.full(key), 1)

            for b in range(B):
                per_head("m1", b, 0, wqT1)
            pe.wait_ge(const_ready, 4)
            for b in range(B):
                per_head("n1T", b, 1, wo1)
                pe.wait_ge(*S.freed(("n1T", b, len(HALVES) - 1)))
                for i, (c0, c1) in enumerate(TCH):
                    transpose_chunks(("n1", b, i), nT, c0, c1, ident)
            pe.wait_ge(*loaded("l2x"))
            bank = acquire(S, "kv2")
            pe.matmul(bank[:, 0:B * R], w2x[:, 1, :], ctxTf, start=True, stop=True)
            pe.matmul(bank[:, B * R:2 * B * R], w2x[:, 2, :], ctxTf, start=True, stop=True).then_inc(S.full("kv2"), 1)
            pe.wait_ge(*loaded("l3x"))
            bank = acquire(S, "k3")
            pe.matmul(bank[:, 0:B * R], w3x[:, 1, :], ctxTf, start=True, stop=True).then_inc(S.full("k3"), 1)
            bank = acquire(S, "m3")
            pe.wait_ge(*S.freed("k3"))
            pe.matmul(bank[:, 0:B * R], w3x[:, 0, :], k3T[:, :], start=True, stop=True)
            pe.matmul(bank[0:1, B * R:2 * B * R], b3x[:, 0:1], k3T[:, :], start=True, stop=True).then_inc(S.full("m3"), 1)
            bank = acquire(S, "v3")
            for b in range(B):
                pe.matmul(bank[0:R, b * D:b * D + D], ctxT[:, b, :], w3x[:, 2, :], start=True, stop=False)
                ins = pe.matmul(bank[0:R, b * D:b * D + D], ones[0:1, 0:R], row_bv3[:, :], start=False, stop=True)
            ins.then_inc(S.full("v3"), 1)
            for b in range(B):
                pe.wait_ge(v2T_ready, b + 1)
                for i, (c0, c1) in enumerate(TCH):
                    transpose_chunks(("v2", b, i), pr[:, b, :], c0, c1, ident)

            for b in range(B):
                transpose_rows("L0x", b)
            pe.wait_ge(m0_ready, 1)
            pe.wait_ge(*S.freed("cb0"))
            for b in range(B):
                bank = acquire(S, ("sim", b))
                pe.wait_ge(*lnT_done("L0x", b))
                for t in range(TB):
                    o = bank[:, t * R:t * R + R]
                    pe.matmul(o, lnT[:, b * TB + t, :], m0[:, b, :], start=True, stop=False)
                    ins = pe.matmul(o, ones[0:1, :], cb0[:, b * R:b * R + R], start=False, stop=True)
                ins.then_inc(S.full(("sim", b)), 1)
            for b in range(B):
                bank = acquire(S, ("hc", b))
                pe.wait_ge(bat_exp, b + 1)
                pe.matmul(bank[:, 0:1], ones[:, :], bat[:, b, 2:3], start=True, stop=True)
                for t in range(TB):
                    ins = pe.matmul(bank[:, 1:2], ln[:, b * TB + t, :], bat[:, b, 8 + t:9 + t],
                                    start=(t == 0), stop=(t == TB - 1))
                ins.then_inc(S.full(("hc", b)), 1)
            for b in range(B):
                bank = acquire(TR, ("aT0", b))
                pe.wait_ge(att_ready, b + 1)
                for t in range(TB):
                    ins = pe.transpose(bank[0:R, t * P:t * P + P], att[:, b, t, :], ident[:, :])
                ins.then_inc(TR.full(("aT0", b)), 1)
            for b in range(B):
                bank = acquire(S, ("hq", b))
                pe.wait_ge(*TR.freed(("aT0", b)))
                pe.matmul(bank[:, :], ctx_rows[:, b, :], attT[:, b, :], start=True, stop=True).then_inc(S.full(("hq", b)), 1)
            pe.wait_ge(*loaded("l0x"))
            for b in range(B):
                bank = acquire(O, ("L0x", b))
                pe.wait_ge(wb0_ready, b + 1)
                pe.wait_ge(*S.freed(("hq", b)))
                pe.wait_ge(prod_ready, b + 1)
                for t in range(TB):
                    o = bank[:, t * D:t * D + D]
                    pe.matmul(o, lnT[:, b * TB + t, :], wb0[:, b, :], start=True, stop=False)
                    pe.matmul(o, hqT[:, b, t * P:t * P + P], wqv0[:, 1, :], start=False, stop=False)
                    pe.matmul(o, prodT[:, b, t * P:t * P + P], wqv0[:, 2, :], start=False, stop=False)
                    ins = pe.matmul(o, ones[0:1, :], row_bqv0[:, :], start=False, stop=True)
                ins.then_inc(O.full(("L0x", b)), 1)

            for b in range(B):
                transpose_rows("L0f", b)
            for b in range(B):
                bank = acquire(S, ("router", b))
                pe.wait_ge(*lnT_done("L0f", b))
                for t in range(TB):
                    ins = pe.matmul(bank[:, t * E:t * E + E], lnT[:, b * TB + t, :], w_router[:, :], start=True, stop=True)
                ins.then_inc(S.full(("router", b)), 1)

            def expert_up(b, k):
                for c in range(C):
                    bank = acquire(S, ("h0", b, k, c))
                    pe.matmul(bank[:, :], experts[:, k, 0, c * P:c * P + P], lnTf[:, b * SEQ:b * SEQ + SEQ],
                              start=True, stop=True).then_inc(S.full(("h0", b, k, c)), 1)

            def expert_down(b, k):
                bank = acquire(O, ("y0", b, k))
                pe.wait_ge(*S.freed(("h0", b, k, C - 1)))
                for t in range(TB):
                    for c in range(C):
                        ins = pe.matmul(bank[:, t * D:t * D + D], hT[:, (b * (E + 1) + k) % 2, c, t * P:t * P + P],
                                        experts[:, k, 1, c * P:c * P + P], start=(c == 0), stop=(c == C - 1))
                ins.then_inc(O.full(("y0", b, k)), 1)

            order = [(b, k) for b in range(B) for k in range(E + 1)]
            for i, (b, k) in enumerate(order):
                if b == 0:
                    pe.wait_ge(*loaded(f"expert{k}"))
                expert_up(b, k)
                if i >= 1:
                    expert_down(*order[i - 1])
                if b == B - 1 and k == 4:
                    transpose_rows("L1x", 0)
            expert_down(*order[-1])

            def attention(layer):
                def scores(n):
                    for i, (h0, h1) in enumerate(HEADS):
                        key = (layer, n, i)
                        bank = acquire(S, key)
                        o = bank[:, 0:(h1 - h0) * R]
                        if layer == "L1x":
                            ins = pe.matmul(o, lnT[:, n, :], m1[:, n // TB, h0 * R:h1 * R], start=True, stop=True)
                        else:
                            pe.matmul(o, q2T[:, n // TB, n % TB * P:(n % TB + 1) * P],
                                      k2blk[:, n // TB, h0:h1, :], start=True, stop=False)
                            ins = pe.matmul(o.rearrange("p (h r) -> p h r", h=h1 - h0), identb[:, :],
                                            penalty[:, n, :].unsqueeze(1).to_broadcast([P, h1 - h0, R]),
                                            start=False, stop=True)
                        ins.then_inc(S.full(key), 1)

                def weighted(n):
                    key = (layer, n // TB)
                    bank = acquire(O, key) if n % TB == 0 else O.bank(key)
                    o = bank[:, n % TB * P:(n % TB + 1) * P]
                    pe.wait_ge(*TR.freed(("pT", layer, n, len(TCH) - 1)))
                    for c in range(CH):
                        k = min(P, HR - c * P)
                        w, v = prT[0:k, n % 2, c, :], (n1 if layer == "L1x" else v2)[0:k, n // TB, c, :]
                        l, r = (w, v) if layer == "L1x" else (v, w)
                        ins = pe.matmul(o, l, r, start=(c == 0), stop=(c == CH - 1))
                    ins.then_inc(O.full(key) if n % TB == TB - 1 else pT_used, 1)

                def project(b):
                    bank = acquire(O, ("o2", b))
                    pe.wait_ge(*O.freed(("L2x", b)))
                    for t in range(TB):
                        o = bank[:, t * D:t * D + D]
                        pe.matmul(o, o2T[:, b, t * P:t * P + P], w2x[:, 3, :], start=True, stop=False)
                        ins = pe.matmul(o, ones[0:1, :], row_bo2[:, :], start=False, stop=True)
                    ins.then_inc(O.full(("o2", b)), 1)

                if layer == "L2x":
                    for b in range(B):
                        bank = acquire(S, ("q2", b))
                        pe.wait_ge(*lnT_done("L2x", b))
                        pe.matmul(bank[:, :], w2x[:, 0, :], lnTf[:, b * SEQ:b * SEQ + SEQ],
                                  start=True, stop=True).then_inc(S.full(("q2", b)), 1)
                    pe.wait_ge(pen_ready, 1)
                    pe.wait_ge(*S.freed(("q2", 1)))
                else:
                    for b in range(B):
                        pe.wait_ge(*lnT_done("L1x", b))
                scores(0)
                for n in range(T):
                    if n + 1 < T:
                        scores(n + 1)
                    pe.wait_ge(p_ready, T * (layer == "L2x") + n + 1)
                    for i, (c0, c1) in enumerate(TCH):
                        transpose_chunks(("pT", layer, n, i), pr[:, n % 2, :], c0, c1, ident)
                    if layer == "L2x" and n == TB + 1:
                        project(0)
                    if n >= 1:
                        weighted(n - 1)
                weighted(T - 1)
                if layer == "L2x":
                    project(1)

            transpose_rows("L1x", 1)
            attention("L1x")
            for b in range(B):
                transpose_quantised("L1f", b)
            pe.wait_ge(wq_ready, 1)
            for b in range(B):
                pe.wait_ge(*TR.freed(("xqT", "L1f", b)))
                for c in range(C):
                    bank = acquire(S, ("h1", b, c))
                    pe.matmul(bank[:, :], fw1q[:, c * P:c * P + P], xqT[:, b * SEQ:b * SEQ + SEQ],
                              start=True, stop=True).then_inc(S.full(("h1", b, c)), 1)
            for b in range(B):
                bank = acquire(O, ("L1f", b))
                pe.wait_ge(hq_ready, b + 1)
                for t in range(TB):
                    n = b * TB + t
                    for c in range(C):
                        ins = pe.matmul(bank[:, t * D:t * D + D], hqb[:, c, n * P:n * P + P], fw2q[:, c, :],
                                        start=(c == 0), stop=(c == C - 1))
                ins.then_inc(O.full(("L1f", b)), 1)
            for b in range(B):
                transpose_rows("L2x", b)
            attention("L2x")
            for b in range(B):
                transpose_quantised("L2f", b)
            for n in range(T + 2):
                if n < T:
                    if n % TB == 0:
                        pe.wait_ge(*TR.freed(("xqT", "L2f", n // TB)))
                    for w, name in enumerate(("gate", "up")):
                        bank = acquire(S, (name, n))
                        pe.matmul(bank[:, :], xqT[:, n * P:n * P + P], guq[:, w, :],
                                  start=True, stop=True).then_inc(S.full((name, n)), 1)
                if 1 <= n <= T:
                    m = n - 1
                    bank = acquire(TR, ("guT", m))[:, :].bitcast(BF16)
                    pe.wait_ge(gub_ready, m + 1)
                    for c in range(C):
                        ins = pe.transpose(bank[:, c * P:c * P + P], gub[:, m % 2, c * P:c * P + P], identb[:, :])
                    ins.then_inc(TR.full(("guT", m)), 1)
                if n >= 2:
                    m = n - 2
                    key = ("L2f", m // TB)
                    bank = acquire(O, key) if m % TB == 0 else O.bank(key)
                    pe.wait_ge(*TR.freed(("guT", m)))
                    for c in range(C):
                        ins = pe.matmul(bank[:, m % TB * D:(m % TB + 1) * D], guT[:, m, c, :], dq[:, c, :],
                                        start=(c == 0), stop=(c == C - 1))
                    if m % TB == TB - 1:
                        ins.then_inc(O.full(key), 1)
            for b in range(B):
                transpose_rows("L3x", b)
            for b in range(B):
                bank = acquire(S, ("s3", b))
                pe.wait_ge(*lnT_done("L3x", b))
                for t in range(TB):
                    o = bank[:, t * R:t * R + R]
                    pe.matmul(o, lnT[:, b * TB + t, :], m3[:, b * R:b * R + R], start=True, stop=False)
                    ins = pe.matmul(o, ones[0:1, :], cb3[:, b * R:b * R + R], start=False, stop=True)
                ins.then_inc(S.full(("s3", b)), 1)
            for b in range(B):
                bank = acquire(TR, ("aT3", b))
                pe.wait_ge(att_ready, B + b + 1)
                for t in range(TB):
                    ins = pe.transpose(bank[0:R, t * P:t * P + P], att[:, b, t, :], ident[:, :])
                ins.then_inc(TR.full(("aT3", b)), 1)
            for b in range(B):
                bank = acquire(O, ("L3x", b))
                pe.wait_ge(*TR.freed(("aT3", b)))
                for t in range(TB):
                    ins = pe.matmul(bank[:, t * D:t * D + D], attT[:, b, t * P:t * P + P], v3[:, b, :],
                                    start=True, stop=True)
                ins.then_inc(O.full(("L3x", b)), 1)
            for b in range(B):
                transpose_rows("L3f", b)
            pe.wait_ge(*loaded("l3f"))
            for b in range(B):
                bank = acquire(S, ("mean", b))
                for t in range(TB):
                    ins = pe.matmul(bank[:, 0:1], ln[:, b * TB + t, :], inv_seq[:, :],
                                    start=(t == 0), stop=(t == TB - 1))
                ins.then_inc(S.full(("mean", b)), 1)
            for b in range(B):
                bank = acquire(S, ("pick", b))
                pe.wait_ge(*S.freed(("mean", b)))
                pe.matmul(bank[0:1, 0:E], mean3[:, b:b + 1], wr3[:, :], start=True, stop=True).then_inc(S.full(("pick", b)), 1)
            for b in range(B):
                pe.wait_ge(pick_ready, b + 1)
                for c in range(C):
                    bank = acquire(S, ("h3", b, c))
                    pe.wait_ge(*lnT_done("L3f", b))
                    pe.matmul(bank[:, :], w1s[:, b, c * P:c * P + P], lnTf[:, b * SEQ:b * SEQ + SEQ],
                              start=True, stop=True).then_inc(S.full(("h3", b, c)), 1)
            for b in range(B):
                bank = acquire(O, ("L3f", b))
                pe.wait_ge(*S.freed(("h3", b, C - 1)))
                for t in range(TB):
                    o = bank[:, t * D:t * D + D]
                    for c in range(C):
                        pe.matmul(o, hT[:, b, c, t * P:t * P + P], w2s[:, b, c * P:c * P + P],
                                  start=(c == 0), stop=False)
                    ins = pe.matmul(o, ones[0:1, :], b2s[:, b, :], start=False, stop=True)
                ins.then_inc(O.full(("L3f", b)), 1)

        @block.vector
        def _(dve):
            steps = [0]

            def step(ins):
                steps[0] += 1
                ins.then_inc(dve_step, 1)
                dve.wait_ge(dve_step, steps[0])

            def normalise(layer, b, ready=True):
                for t in range(b * TB, b * TB + TB):
                    ins = dve.bn_stats(bn[:, t, :], x[:, t, :])
                step(ins)
                for t in range(b * TB, b * TB + TB):
                    ins = dve.bn_aggr(mv[:, t, :], bn[:, t, :])
                step(ins)
                y, sq = rstd[:, b * TB:b * TB + TB], newton[:, b, 2, :]
                dve.tensor_scalar(newton[:, b, 1, :], mv[:, b * TB:b * TB + TB, 1], EPS, -0.5, ALU.add, ALU.mult)
                step(dve.tensor_scalar(newton[:, b, 0, :], mv[:, b * TB:b * TB + TB, 1], EPS, 0.5, ALU.add, ALU.mult))
                step(dve.tensor_scalar(y.bitcast(I32), newton[:, b, 0, :].bitcast(I32), -0.5, GUESS, ALU.mult, ALU.add))
                for _ in range(3):
                    step(dve.tensor_tensor(sq, y, y, ALU.mult))
                    step(dve.tensor_tensor(sq, sq, newton[:, b, 1, :], ALU.mult))
                    step(dve.scalar_tensor_tensor(y, sq, 1.5, y, ALU.add, ALU.mult))
                for t in range(b * TB, b * TB + TB):
                    ins = dve.tensor_scalar(ln[:, t, :], x[:, t, :], mv[:, t, 0:1], rstd[:, t:t + 1],
                                            ALU.subtract, ALU.mult)
                ins.then_inc(ln_ready, 1)

            def update(key, b, gate, src=None):
                rows = x[:, b * TB:b * TB + TB, :]
                dve.wait_ge(*O.filled(key))
                dve.scalar_tensor_tensor(rows, O.bank(key)[:, :].rearrange("p (t d) -> p t d", t=TB),
                                         G[:, gate:gate + 1], rows, ALU.mult, ALU.add).then_inc(O.free(key), 1)
                dve.wait_ge(*O.freed(key))

            def bc(v, n):
                return v.unsqueeze(2).to_broadcast([P, v.shape[1], n])

            dve.wait_ge(*loaded("ctx"))
            dve.tensor_scalar(m0[:, :, :], ctxT[:, :, :], simw[:, 2:3], simw[:, 0:1], ALU.mult, ALU.add).then_inc(m0_ready, 1)
            dve.wait_ge(*S.filled("cb0"))
            dve.tensor_scalar(cb0[:, :], S.bank("cb0")[0:1, 0:B * R], b_sim[:, 0:1], None, ALU.add).then_inc(S.free("cb0"), 1)
            dve.wait_ge(*S.freed("cb0"))
            dve.wait_ge(*loaded("mask"))
            dve.tensor_scalar(penalty[:, :, :], mask[:, :, :], 0.0, MASKED, ALU.is_equal, ALU.mult).then_inc(pen_ready, 1)
            dve.wait_ge(*loaded("x0"))
            normalise("L0x", 0)
            dve.wait_ge(*loaded("x1"))
            normalise("L0x", 1)
            dve.wait_ge(*S.freed("kv2"))
            dve.wait_ge(const_ready, 4)
            for b in range(B):
                m = headmask[:, :].unsqueeze(2).to_broadcast([P, H, R])

                def blocks(w):
                    return kv2T[:, w, b * R:b * R + R].unsqueeze(1).to_broadcast([P, H, R])
                dve.tensor_tensor(k2blk[:, b, :, :], blocks(0), m, ALU.mult)
                dve.tensor_tensor(pr[:, b, :].rearrange("p (h r) -> p h r", h=H), blocks(1), m,
                                  ALU.mult).then_inc(v2T_ready, 1)

            def softmax_in(bank_key, b):
                v = S.bank(bank_key)[:, 0:TB * R].rearrange("p (t r) -> p t r", t=TB)
                dve.wait_ge(*S.filled(bank_key))
                step(dve.tensor_reduce(amax[:, b, :], v, AX, ALU.max))
                dve.tensor_tensor(att[:, b, :, :], v, bc(amax[:, b, :], R), ALU.subtract).then_inc(S.free(bank_key), 1)

            def softmax_out(b, count):
                dve.wait_ge(att_exp, count)
                step(dve.tensor_reduce(asum[:, b, :], att[:, b, :, :], AX, ALU.add))
                step(dve.reciprocal(asum[:, b, :], asum[:, b, :]))
                dve.tensor_tensor(att[:, b, :, :], att[:, b, :, :], bc(asum[:, b, :], R), ALU.mult).then_inc(att_ready, 1)

            for b in range(B):
                softmax_in(("sim", b), b)
                dve.tensor_reduce(bat[:, b, 0:1], amax[:, b, :], AX, ALU.max).then_inc(bmax_ready, 1)
            for b in range(B):
                dve.wait_ge(bmax_all, b + 1)
                dve.tensor_scalar(bat[:, b, 8:12], amax[:, b, :], bat[:, b, 1:2], None, ALU.subtract).then_inc(bat_sub, 1)
            for b in range(B):
                softmax_out(b, b + 1)
            dve.wait_ge(*loaded("l0x"))
            for b in range(B):
                dve.wait_ge(*S.filled(("hc", b)))
                step(dve.reciprocal(bat[:, b, 3:4], S.bank(("hc", b))[:, 0:1]))
                dve.tensor_scalar(bat[:, b, 4:5], S.bank(("hc", b))[:, 1:2], bat[:, b, 3:4], None,
                                  ALU.mult).then_inc(S.free(("hc", b)), 1)
                dve.wait_ge(*S.freed(("hc", b)))
                dve.scalar_tensor_tensor(wb0[:, b, :], wqv0[:, 3, :], bat[:, b, 4:5], wqv0[:, 0, :], ALU.mult,
                                         ALU.add).then_inc(wb0_ready, 1)
            for b in range(B):
                dve.wait_ge(*S.freed(("hq", b)))
                dve.tensor_tensor(prodT[:, b, :], hqT[:, b, :], lnTf[:, b * SEQ:b * SEQ + SEQ],
                                  ALU.mult).then_inc(prod_ready, 1)
            dve.wait_ge(gates_ready, 1)
            for b in range(B):
                update(("L0x", b), b, 0)
                normalise("L0f", b)

            for b in range(B):
                key = ("router", b)
                dve.wait_ge(*S.filled(key))
                dve.tensor_copy(logits[:, b, :, :], S.bank(key)[:, 0:TB * E].rearrange("p (t e) -> p t e", t=TB)).then_inc(S.free(key), 1)
                dve.wait_ge(*S.freed(key))
                for t in range(TB):
                    ins = dve.max(top[:, b, t, :], logits[:, b, t, :])
                step(ins)
                for t in range(TB):
                    dve.max_index(topi[:, b, t, :], top[:, b, t, :], logits[:, b, t, :])
                dve.tensor_tensor(tw[:, b, 0, :], top[:, b, :, 1], top[:, b, :, 0], ALU.subtract).then_inc(gap_ready, 1)
            for b in range(B):
                step(dve.tensor_copy(topf[:, b, :, :], topi[:, b, :, :]))
                dve.wait_ge(gap_exp, b + 1)
                step(dve.tensor_scalar(tw[:, b, 2, :], tw[:, b, 1, :], 1.0, None, ALU.add))
                step(dve.reciprocal(tw[:, b, 2, :], tw[:, b, 2, :]))
                step(dve.tensor_tensor(tw[:, b, 3, :], tw[:, b, 1, :], tw[:, b, 2, :], ALU.mult))
                for t in range(TB):
                    dve.tensor_scalar(cw[:, b, t, :], iota8[:, :], topf[:, b, t, 0:1], tw[:, b, 2, t:t + 1],
                                      ALU.is_equal, ALU.mult)
                    ins = dve.tensor_scalar(cw2[:, b, t, :], iota8[:, :], topf[:, b, t, 1:2], tw[:, b, 3, t:t + 1],
                                            ALU.is_equal, ALU.mult)
                step(ins)
                step(dve.tensor_tensor(cw[:, b, :, :], cw[:, b, :, :], cw2[:, b, :, :], ALU.add))

            def weight_stats():
                dve.wait_ge(*loaded("l1f"))
                dve.wait_ge(*loaded("l2f"))
                for i, (w, op) in enumerate(((fw1[:, :], ALU.max), (flat(fw2), ALU.max), (fw_gu[:, 0, :], ALU.add),
                                             (fw_gu[:, 1, :], ALU.add), (flat(fw_d), ALU.add))):
                    ins = dve.tensor_reduce(wstat[:, i:i + 1], w, AX, op, apply_absolute_value=True)
                ins.then_inc(wstat_ready, 1)

            def weight_quantise():
                dve.wait_ge(wall_ready, 1)
                step(dve.tensor_scalar(wsc[:, 0:2], wall[:, 0:2], 1e-6, 1.0 / QP, ALU.max, ALU.mult))
                step(dve.reciprocal(wsc[:, 12:14], wsc[:, 0:2]))
                step(dve.tensor_scalar(wsc[:, 14:17], wall[:, 2:5], 1.0 / (D * FF), 1e-5, ALU.mult, ALU.max))
                step(dve.reciprocal(wsc[:, 17:20], wsc[:, 14:17]))
                for i, w in enumerate((fw1[:, :], flat(fw2))):
                    ins = dve.tensor_scalar(w, w, wsc[:, 12 + i:13 + i], MAGIC, ALU.mult, ALU.add)
                ws = (fw_gu[:, 0, :], fw_gu[:, 1, :], flat(fw_d))
                for i, w in enumerate(ws):
                    ins = dve.tensor_scalar(w, w, wsc[:, 17 + i:18 + i], 1.0, ALU.mult, ALU.min)
                step(ins)
                for w in ws:
                    ins = dve.tensor_scalar(w, w, -1.0, MAGIC, ALU.max, ALU.add)
                step(ins)
                for w, q in ((fw1[:, :], fw1q[:, :]), (flat(fw2), flat(fw2q)), (fw_gu[:, 0, :], guq[:, 0, :]),
                             (fw_gu[:, 1, :], guq[:, 1, :]), (flat(fw_d), flat(dq))):
                    ins = dve.tensor_scalar(q, w, MAGIC, None, ALU.subtract)
                ins.then_inc(wq_ready, 1)

            for b in range(B):
                for k in range(E + 1):
                    key = ("y0", b, k)
                    dve.wait_ge(*O.filled(key))
                    y = O.bank(key)[:, :].rearrange("p (t d) -> p t d", t=TB)
                    if k == 0:
                        dve.tensor_copy(acc[:, b, :, :], y).then_inc(O.free(key), 1)
                    else:
                        dve.wait_ge(*O.freed(("y0", b, k - 1)))
                        for t in range(TB):
                            ins = dve.scalar_tensor_tensor(acc[:, b, t, :], y[:, t, :], cw[:, b, t, k - 1:k],
                                                           acc[:, b, t, :], ALU.mult, ALU.add)
                        ins.then_inc(O.free(key), 1)
                    if b == 0 and k == 3:
                        weight_stats()
                    if b == 0 and k == 5:
                        weight_quantise()
                    if b == 1 and k == 2:
                        normalise("L1x", 0)
                dve.wait_ge(*O.freed(("y0", b, E)))
                rows = x[:, b * TB:b * TB + TB, :]
                step(dve.scalar_tensor_tensor(rows, acc[:, b, :, :], G[:, 4:5], rows, ALU.mult, ALU.add))
            normalise("L1x", 1)

            def attention(layer, finish):
                base = T * (layer == "L2x")

                def less_max(n):
                    if n >= 2:
                        dve.wait_ge(*TR.filled(("pT", layer, n - 2, len(TCH) - 1)))
                    for i, (h0, h1) in enumerate(HEADS):
                        key = (layer, n, i)
                        v = S.bank(key)[:, 0:(h1 - h0) * R].rearrange("p (h r) -> p h r", h=h1 - h0)
                        dve.wait_ge(*S.filled(key))
                        step(dve.tensor_reduce(pmax[:, n % 2, h0:h1], v, AX, ALU.max))
                        dve.tensor_tensor(pr[:, n % 2, h0 * R:h1 * R].rearrange("p (h r) -> p h r", h=h1 - h0), v,
                                          bc(pmax[:, n % 2, h0:h1], R), ALU.subtract).then_inc(S.free(key), 1)

                less_max(0)
                for n in range(T):
                    if n + 1 < T:
                        less_max(n + 1)
                    dve.wait_ge(p_exp, base + n + 1)
                    step(dve.tensor_reduce(psums[:, n % 2, 0, :], pr[:, n % 2, :].rearrange("p (h r) -> p h r", h=H),
                                           AX, ALU.add))
                    dve.reciprocal(psums[:, n % 2, 1, :], psums[:, n % 2, 0, :]).then_inc(p_recip, 1)
                    if n == TB + 2:
                        finish(0)
                finish(1)

            def finish_l1x(b):
                update(("L1x", b), b, 1)
                normalise("L1f", b)
                dve.wait_ge(*ln_done("L1f", b))
                step(dve.tensor_reduce(hmax[:, 2 * b:2 * b + 1], ln[:, b * TB:b * TB + TB, :].rearrange("p t d -> p (t d)"),
                                       AX, ALU.max, apply_absolute_value=True))

            attention("L1x", finish_l1x)
            dve.tensor_tensor(hmax[:, B * C:B * C + 1], hmax[:, 0:1], hmax[:, 2:3], ALU.max).then_inc(amax_ready, 1)
            dve.wait_ge(amax_all, 1)
            step(dve.tensor_scalar(wsc[:, 3:4], hall[:, 0:1], 1e-6, 1.0 / QP, ALU.max, ALU.mult))
            step(dve.reciprocal(wsc[:, 8:9], wsc[:, 3:4]))
            for b in range(B):
                rows = ln[:, b * TB:b * TB + TB, :]
                q = qtmp[:, b, :, :]
                step(dve.tensor_scalar(q, rows, wsc[:, 8:9], MAGIC, ALU.mult, ALU.add))
                dve.tensor_scalar(xqb[:, b * TB:b * TB + TB, :], q, MAGIC, None, ALU.subtract).then_inc(xq_ready, 1)
            step(dve.tensor_tensor(wsc[:, 2:3], wsc[:, 3:4], wsc[:, 0:1], ALU.mult))
            dve.tensor_scalar(wsc[:, 4:8], fb1[:, :], wsc[:, 2:3], None, ALU.mult).then_inc(s1_ready, 1)
            for b in range(B):
                for c in range(C):
                    dve.wait_ge(*S.freed(("h1", b, c)))
                    ins = dve.tensor_reduce(hmax[:, b * C + c:b * C + c + 1], hT[:, b, c, :], AX, ALU.max,
                                            apply_absolute_value=True)
            step(ins)
            dve.tensor_reduce(hmax[:, B * C + 1:B * C + 2], hmax[:, 0:B * C], AX, ALU.max).then_inc(amax_ready, 1)
            dve.wait_ge(amax_all, 2)
            step(dve.tensor_scalar(wsc[:, 9:10], hall[:, 1:2], 1e-6, 1.0 / QP, ALU.max, ALU.mult))
            step(dve.reciprocal(wsc[:, 10:11], wsc[:, 9:10]))
            for b in range(B):
                v = hT[:, b, :, :]
                step(dve.tensor_scalar(v, v, wsc[:, 10:11], MAGIC, ALU.mult, ALU.add))
                dve.tensor_scalar(hqb[:, :, b * SEQ:b * SEQ + SEQ], v, MAGIC, None, ALU.subtract).then_inc(hq_ready, 1)
            step(dve.tensor_scalar(wsc[:, 11:12], wsc[:, 9:10], wsc[:, 1:2], G[:, 5:6], ALU.mult, ALU.mult))
            for b in range(B):
                key = ("L1f", b)
                q, rows = qtmp[:, b, :, :], x[:, b * TB:b * TB + TB, :]
                dve.wait_ge(*O.filled(key))
                dve.tensor_tensor(q, O.bank(key)[:, :].rearrange("p (t d) -> p t d", t=TB),
                                  b2_1[:, :].unsqueeze(1).to_broadcast([P, TB, D]), ALU.add).then_inc(O.free(key), 1)
                dve.wait_ge(*O.freed(key))
                step(dve.scalar_tensor_tensor(rows, q, wsc[:, 11:12], rows, ALU.mult, ALU.add))
                normalise("L2x", b)

            def finish_l2x(b):
                ts = slice(b * TB, b * TB + TB)
                update(("o2", b), b, 2)
                normalise("L2f", b)
                dve.wait_ge(*ln_done("L2f", b))
                step(dve.tensor_reduce(tsc[:, 0, ts], ln[:, ts, :], AX, ALU.max, apply_absolute_value=True))
                step(dve.tensor_scalar(tsc[:, 0, ts], tsc[:, 0, ts], 1e-5, 1.0 / QP, ALU.max, ALU.mult))
                step(dve.reciprocal(tsc[:, 1, ts], tsc[:, 0, ts]))
                for t in range(TB):
                    n = b * TB + t
                    ins = dve.tensor_scalar(qtmp[:, b, t, :], ln[:, n, :], tsc[:, 1, n:n + 1], MAGIC, ALU.mult, ALU.add)
                step(ins)
                dve.tensor_scalar(xqb[:, ts, :], qtmp[:, b, :, :], MAGIC, QP, ALU.subtract, ALU.min).then_inc(xq_ready, 1)
                dve.tensor_scalar(tsc[:, 3, ts], tsc[:, 0, ts], wsc[:, 15:16], None, ALU.mult)
                dve.tensor_scalar(tsc[:, 2, ts], tsc[:, 0, ts], wsc[:, 14:15], None, ALU.mult).then_inc(tscale_ready, 1)

            attention("L2x", finish_l2x)
            def down_update(m):
                key = ("L2f", m // TB)
                ins = dve.scalar_tensor_tensor(x[:, m, :], O.bank(key)[:, m % TB * D:(m % TB + 1) * D], tsc[:, 6, m:m + 1],
                                               x[:, m, :], ALU.mult, ALU.add)
                return ins

            for n in range(T):
                if n >= 2:
                    dve.wait_ge(*TR.filled(("guT", n - 2)))
                dve.wait_ge(*S.filled(("up", n)))
                dve.wait_ge(*S.freed(("gate", n)))
                g = guf[:, n % 2, :]
                dve.scalar_tensor_tensor(g, S.bank(("up", n))[:, :], tsc[:, 3, n:n + 1], silu[:, n % 2, :],
                                         ALU.mult, ALU.mult).then_inc(S.free(("up", n)), 1)
                dve.wait_ge(*S.freed(("up", n)))
                step(dve.tensor_reduce(tsc[:, 4, n:n + 1], g, AX, ALU.max, apply_absolute_value=True))
                step(dve.tensor_scalar(tsc[:, 4, n:n + 1], tsc[:, 4, n:n + 1], 1e-5, 1.0 / QP, ALU.max, ALU.mult))
                step(dve.reciprocal(tsc[:, 5, n:n + 1], tsc[:, 4, n:n + 1]))
                dve.tensor_scalar(tsc[:, 6, n:n + 1], tsc[:, 4, n:n + 1], wsc[:, 16:17], G[:, 6:7], ALU.mult, ALU.mult)
                step(dve.tensor_scalar(g, g, tsc[:, 5, n:n + 1], MAGIC, ALU.mult, ALU.add))
                dve.tensor_scalar(gub[:, n % 2, :], g, MAGIC, QP, ALU.subtract, ALU.min).then_inc(gub_ready, 1)
            for b in range(B):
                key = ("L2f", b)
                dve.wait_ge(*O.filled(key))
                for m in range(b * TB, b * TB + TB):
                    ins = down_update(m)
                ins.then_inc(O.free(key), 1)
                dve.wait_ge(*O.freed(key))
                normalise("L3x", b)

            for b in range(B):
                softmax_in(("s3", b), b)
            for b in range(B):
                softmax_out(b, B + b + 1)
            for b in range(B):
                update(("L3x", b), b, 3)
                normalise("L3f", b)
            for b in range(B):
                dve.wait_ge(*S.filled(("mean", b)))
                dve.tensor_copy(mean3[:, b:b + 1], S.bank(("mean", b))[:, 0:1]).then_inc(S.free(("mean", b)), 1)
            dve.wait_ge(*loaded("l3f"))
            for b in range(B):
                key = ("pick", b)
                dve.wait_ge(*S.filled(key))
                dve.tensor_tensor(sc3[:, b, :], S.bank(key)[0:1, 0:E], br3[:, :], ALU.add).then_inc(S.free(key), 1)
                dve.wait_ge(*S.freed(key))
                step(dve.max(top3[:, b, :], sc3[:, b, :]))
                step(dve.max_index(top3i[:, b, :], top3[:, b, :], sc3[:, b, :]))
                e = dve.value_load(top3i[0:1, b, 0:1], min_val=0, max_val=E - 1)
                dve.tensor_copy(w1s[:, b, :], ex_flat[:, bass.ds(e * (2 * FF), FF)])
                dve.tensor_copy(w2s[:, b, :], ex_flat[:, bass.ds(e * (2 * FF) + FF, FF)])
                dve.tensor_copy(b2s[:, b, :], b2_flat[:, bass.ds(e * D, D)])
                dve.tensor_copy(b1s[:, b, :], b1_flat[:, bass.ds(e * C, C)]).then_inc(pick_ready, 1)
            for b in range(B):
                rows, key = x[:, b * TB:b * TB + TB, :], ("L3f", b)
                dve.wait_ge(*O.filled(key))
                dve.scalar_tensor_tensor(rows, O.bank(key)[:, :].rearrange("p (t d) -> p t d", t=TB), G[:, 7:8],
                                         rows, ALU.mult, ALU.add).then_inc(x_final, 1)


def layout(i):
    def rows(w, n):
        return w.reshape(n, 128, -1).transpose(1, 0, 2)

    f = {k: np.asarray(v) for k, v in i.items()}
    c = f["ctx_1024"]
    w1 = np.concatenate([f["L0_ffn_w1_shared"][None], f["L0_ffn_w1_routed"]])
    w2 = np.concatenate([f["L0_ffn_w2_shared"][None], f["L0_ffn_w2_routed"]])
    return {
        "x": f["x"], "mask": f["mask_Bx1xSxS2_if1"][:, 0],
        "ctxT": c.transpose(2, 0, 1), "ctx_rows": c.transpose(1, 0, 2),
        "g_xattn": f["g_xattn"], "g_ffn": f["g_ffn"],
        "simw": f["L0_xattn_w_sim"].reshape(3, 128).T, "b_sim": f["L0_xattn_b_sim"].reshape(1, 1),
        "wqv0": rows(f["L0_xattn_W_qv"], 4), "bqv0": f["L0_xattn_b_qv"][None],
        "w_router": f["L0_ffn_w_router"], "w1_0": w1.transpose(1, 0, 2),
        "w2_0": w2.reshape(9, 4, 128, 128).transpose(2, 0, 1, 3).reshape(128, 9, 512),
        "wqT1": rows(f["L1_xattn_Wq"].T, 8), "wk1": f["L1_xattn_Wk"], "wv1": f["L1_xattn_Wv"],
        "wo1": rows(f["L1_xattn_Wo"], 8),
        "fw1": f["L1_ffn_w1"].T, "fb1": f["L1_ffn_b1"].reshape(4, 128).T, "fw2": rows(f["L1_ffn_w2"].T, 4),
        "b2_1": f["L1_ffn_b2"],
        "w2x": np.stack([f["L2_xattn_W" + k].T for k in "qkvo"], axis=1), "bo2": f["L2_xattn_bo"][None],
        "fw_gu": np.stack([f["L2_ffn_w_gate"].T, f["L2_ffn_w_up"].T], axis=1), "fw_d": rows(f["L2_ffn_w_down"].T, 4),
        "w3x": np.stack([f["L3_xattn_Wq"], f["L3_xattn_Wk"].T, f["L3_xattn_Wv"].T], axis=1),
        "b3x": np.stack([f["L3_xattn_bq"], f["L3_xattn_bk"]], axis=1), "bv3": f["L3_xattn_bv"][None],
        "wr3": f["L3_ffn_Wr"], "br3": f["L3_ffn_br"][None], "w1_3": f["L3_ffn_W1"].transpose(1, 0, 2),
        "b1_3": f["L3_ffn_b1"].reshape(8, 4, 128).transpose(2, 0, 1),
        "w2_3": f["L3_ffn_W2"].reshape(8, 4, 128, 128).transpose(2, 0, 1, 3).reshape(128, 8, 512),
        "b2_3": f["L3_ffn_b2"].reshape(1, -1),
    }


def kernel(**inputs):
    import concourse.bacc as bacc
    from concourse.bass_utils import run_bass_kernel_spmd

    nc = bacc.Bacc("TRN2", target_bir_lowering=False, num_devices=1)
    arrays, args = {}, {}
    for name, v in layout(inputs).items():
        v = np.ascontiguousarray(v)
        arrays["in_" + name] = v
        args[name] = nc.dram_tensor("in_" + name, v.shape, mybir.dt.from_np(v.dtype), kind="ExternalInput").ap()
    out = nc.dram_tensor("out_x", (B, SEQ, D), F32, kind="ExternalOutput").ap()
    program(nc, args, out)
    r = run_bass_kernel_spmd(nc, [arrays], core_ids=[0])
    return r.results[0]["out_x"]
```

```python
from contextlib import ExitStack

import numpy as np
import concourse.bass as bass
from concourse import mybir

ALU = mybir.AluOpType
ACT = mybir.ActivationFunctionType
F32 = mybir.dt.float32
BF16 = mybir.dt.bfloat16
F32R = mybir.dt.float32r
I32 = mybir.dt.int32
U32 = mybir.dt.uint32
AX = mybir.AxisListType.X
RMAX = bass.bass_isa.ReduceOp.max
RADD = bass.bass_isa.ReduceOp.add

P = 128
B, SEQ, D = 2, 512, 128
TB = SEQ // P
T = B * TB
R = 77
E = 8
FF = 512
C = FF // P
H = 16
HR = H * R
CH = -(-HR // P)
HB = 512 // R
HEADS = [(h, min(h + HB, H)) for h in range(0, H, HB)]
DH1, DH2 = 64, D // H
NK1 = H * DH1 // P
HALVES = [(h, min(h + 3, half + H // 2)) for half in (0, H // 2) for h in range(half, half + H // 2, 3)]
TCH = [(c, min(c + 4, CH)) for c in range(0, CH, 4)]
EPS = 1e-5
MAGIC = 1.5 * 2.0 ** 23
MASKED = -(2.0 ** 100)
GUESS = 1593268703.0
QP = 127.0
LAYERS = ["L0x", "L0f", "L1x", "L1f", "L2x", "L2f", "L3x", "L3f"]


class Ring:

    def __init__(self, banks, full, free, keys):
        self.banks, self.full_sems, self.free_sems = banks, full, free
        self.use = {k: (i % len(banks), i // len(banks)) for i, k in enumerate(keys)}
        assert len(self.use) == len(keys)

    def bank(self, key):
        return self.banks[self.use[key][0]]

    def full(self, key):
        return self.full_sems[self.use[key][0]]

    def free(self, key):
        return self.free_sems[self.use[key][0]]

    def reused(self, key):
        return self.use[key][1] > 0

    def freed_before(self, key):
        return self.free(key), self.use[key][1]

    def filled(self, key):
        return self.full(key), self.use[key][1] + 1

    def freed(self, key):
        return self.free(key), self.use[key][1] + 1


def bank_keys():
    s = ["cb0"]
    o = []
    t = [("lnT", "L0x", b) for b in range(B)]
    s += [("kv1", 0, i) for i in range(3)]
    s += [("sim", b) for b in range(B)]
    s += [("kv1", 1, i) for i in range(3)]
    s += [("m1", i) for i in range(len(HALVES))]
    s += [("hc", b) for b in range(B)]
    t += [("aT0", b) for b in range(B)]
    s += [("hq", b) for b in range(B)]
    o += [("L0x", b) for b in range(B)]
    s += [("n1T", i) for i in range(len(HALVES))]
    s += ["kv2", "k3", "m3", "v3"]
    t += [("n1", b, i) for b in range(B) for i in range(len(TCH))]
    t += [("lnT", "L0f", b) for b in range(B)]
    s += [("router", b) for b in range(B)]
    t += [("v2", b, i) for b in range(B) for i in range(len(TCH))]
    for b in range(B):
        for e in range(E + 1):
            s += [("h0", b, e, c) for c in range(C)]
            o.append(("y0", b, e))
    for layer in ("L1x", "L2x"):
        t += [("lnT", layer, b) for b in range(B)]
        for n in range(T):
            if layer == "L2x" and n < B:
                s.append(("q2", n))
            s += [(layer, n, i) for i in range(len(HEADS))]
        for n in range(T):
            t += [("pT", layer, n, i) for i in range(len(TCH))]
            if n % TB == 0:
                o.append((layer, n // TB))
            if n % TB == TB - 1 and layer == "L2x":
                o.append(("o2", n // TB))
        if layer == "L1x":
            t += [("xqT", "L1f", b) for b in range(B)]
            s += [("h1", b, c) for b in range(B) for c in range(C)]
            o += [("L1f", b) for b in range(B)]
    t += [("xqT", "L2f", b) for b in range(B)]
    s += [(w, n) for n in range(T) for w in ("gate", "up")]
    t += [("guT", n) for n in range(T)]
    o += [("L2f", b) for b in range(B)]
    t += [("lnT", "L3x", b) for b in range(B)]
    s += [("s3", b) for b in range(B)]
    t += [("aT3", b) for b in range(B)]
    o += [("L3x", b) for b in range(B)]
    t += [("lnT", "L3f", b) for b in range(B)]
    s += [("mean", b) for b in range(B)]
    s += [("pick", b) for b in range(B)]
    s += [("h3", b, c) for b in range(B) for c in range(C)]
    o += [("L3f", b) for b in range(B)]
    return s, t, o


def program(nc, a, out):
    ctx = ExitStack()
    with ctx:
        def sb(name, shape, dt=F32):
            return ctx.enter_context(nc.sbuf_tensor(name, shape, dt))

        def sem(name):
            return ctx.enter_context(nc.semaphore(name))

        x = sb("x", [P, T, D])
        ctx_rows = sb("ctx_rows", [R, B, D])
        ctxT = sb("ctxT", [P, B, R])
        gates = sb("gates", [P, 8])
        simw = sb("simw", [P, 3])
        b_sim = sb("b_sim", [1, 1])
        wqv0 = sb("wqv0", [P, 4, D])
        bqv0 = sb("bqv0", [P, D])
        bo2 = sb("bo2", [P, D])
        row_bv3 = sb("row_bv3", [1, D])
        w_router = sb("w_router", [P, E])
        experts = sb("experts", [P, E + 1, 2, FF])
        wqT1 = sb("wqT1", [P, H * DH1 // P, D])
        wkv1 = sb("wkv1", [P, 2, H * DH1])
        wo1 = sb("wo1", [P, H * DH1 // P, D])
        fw1 = sb("fw1", [P, FF])
        fb1 = sb("fb1", [P, C])
        fw2 = sb("fw2", [P, C, D])
        b2_1 = sb("b2_1", [P, D])
        w2x = sb("w2x", [P, 4, D])
        fw_gu = sb("fw_gu", [P, 2, FF])
        fw_d = sb("fw_d", [P, C, D])
        w3x = sb("w3x", [P, 3, D])
        b3x = sb("b3x", [P, 2])
        wr3 = sb("wr3", [P, E])
        br3 = sb("br3", [1, E])
        b1_3 = sb("b1_3", [P, E, C])

        ident = sb("ident", [P, P])
        identb = sb("identb", [P, P], BF16)
        ones = sb("ones", [P, P])
        iota8 = sb("iota8", [P, E])
        headmask = sb("headmask", [P, H])
        inv_seq = sb("inv_seq", [P, 1])
        magic = sb("magic", [P, 1])
        G = sb("G", [P, 8])

        m0 = sb("m0", [P, B, R])
        cb0 = sb("cb0_row", [1, B * R])
        m1 = sb("m1", [P, B, HR])
        n1 = sb("n1", [P, B, CH, D])
        kv2T = sb("kv2T", [P, 2, B * R])
        k2blk = sb("k2blk", [P, B, H, R])
        v2 = sb("v2", [P, B, CH, D])
        k3T = sb("k3T", [P, B * R])
        m3 = sb("m3", [P, B * R])
        cb3 = sb("cb3_row", [1, B * R])
        v3 = sb("v3", [R, B, D])
        penalty = sb("penalty", [P, T, R], BF16)
        fw1q = sb("fw1q", [P, FF], BF16)
        fw2q = sb("fw2q", [P, C, D], BF16)
        guq = sb("guq", [P, 2, FF], BF16)
        dq = sb("dq", [P, C, D], BF16)
        wstat = sb("wstat", [P, 8])
        wall = sb("wall", [P, 8])
        wsc = sb("wsc", [P, 20])

        bn = sb("bn", [P, T, 6])
        mv = sb("mv", [P, T, 2])
        rstd = sb("rstd", [P, T])
        newton = sb("newton", [P, B, 3, TB])
        ln = sb("ln", [P, T, D])
        lnT = sb("lnT", [P, T, P])
        lnTf = lnT[:, :, :].rearrange("p t n -> p (t n)")
        att_all = sb("att_all", [P, B * TB * (R + P)])
        att = att_all[:, 0:B * TB * R].rearrange("p (b t r) -> p b t r", b=B, t=TB)
        attT = att_all[0:R, B * TB * R:].rearrange("r (b n) -> r b n", b=B)
        amax = sb("amax", [P, B, TB])
        asum = sb("asum", [P, B, TB])
        hq_prod = sb("hq_prod", [P, 2, B, TB * P])
        hqT, prodT = hq_prod[:, 0, :, :], hq_prod[:, 1, :, :]
        bat = sb("bat", [P, B, 12])
        wb0 = sb("wb0", [P, B, D])
        logits = sb("logits", [P, B, TB, E])
        top = sb("top", [P, B, TB, 8])
        topi = sb("topi", [P, B, TB, 8], U32)
        topf = sb("topf", [P, B, TB, 8])
        tw = sb("tw", [P, B, 4, TB])
        cw = sb("cw", [P, B, TB, E])
        cw2 = sb("cw2", [P, B, TB, E])
        hT = sb("hT", [P, 2, C, TB * P])
        acc = sb("acc", [P, B, TB, D])
        pmax = sb("pmax", [P, 4, H])
        psums = sb("psums", [P, 4, 2, H])
        xqb = sb("xqb", [P, T, D], BF16)
        xqT = sb("xqT", [P, T * P], BF16)
        hmax = sb("hmax", [P, B * C + 2])
        hall = sb("hall", [P, 2])
        tsc = sb("tsc", [P, 8, T])
        gub = sb("gub", [P, 2, FF], BF16)
        mean3 = sb("mean3", [P, B])
        sc3 = sb("sc3", [1, B, 8])
        top3 = sb("top3", [1, B, 8])
        top3i = sb("top3i", [1, B, 8], U32)
        b1s = sb("b1s", [P, B, C])
        with ExitStack() as split:
            w1S = split.enter_context(nc.sbuf_tensor("w1S", [P, 2, 2, FF], F32R))
            lnS = split.enter_context(nc.sbuf_tensor("lnS", [P, 2, T * P], F32R))
        pr = sb("pr", [P, 3, HR])
        prT = sb("prT", [P, 2, CH, P])
        kv1T = hT[:, :, :, :].rearrange("p n c k -> p (n c k)")[:, 0:2 * NK1 * B * R].rearrange(
            "p (w c r) -> p w c r", w=2, c=NK1)
        silu = pr[:, :, 0:FF]
        guf = prT[:, :, 0:C, :].rearrange("p n c k -> p n (c k)")
        hqb = wkv1[:, :, :].rearrange("p w n -> p (w n)").bitcast(BF16).rearrange("p (c n) -> p c n", c=C)
        guT = hqb[:, :, :].rearrange("p c n -> p (c n)").rearrange("p (t c k) -> p t c k", t=T, c=C)
        qtmp = wqT1[:, :, :].rearrange("p (b t) d -> p b t d", b=B)
        b2s = wb0[0:1, :, :]
        mask = att_all[:, 0:B * TB * R].rearrange("p (n r) -> p n r", r=R).bitcast(I32)
        q2T = hqT
        o2T = hqT
        w1s = prodT
        w2s = acc[:, :, :, :].rearrange("p b t d -> p b (t d)")
        ctxTf = ctxT[:, :, :].rearrange("p b r -> p (b r)")
        ex_flat = experts[:, :, :, :].rearrange("p e w n -> p (e w n)")
        b1_flat = b1_3[:, :, :].rearrange("p e c -> p (e c)")
        nT = pr[:, 1:1 + B, :]
        pr4 = [pr[:, 0, :], pr[:, 1, :], pr[:, 2, :], att_all[:, 0:HR]]
        v2T = [wkv1[:, :, :].rearrange("p w n -> p (w n)")[:, 0:HR],
               hq_prod[:, :, :, :].rearrange("p w b n -> p (w b n)")[:, 0:HR]]
        b2_flat = m1[:, :, :].rearrange("p b n -> p (b n)")[0:1, 0:E * D]

        def flat(w):
            return w[:, :, :].rearrange("p c k -> p (c k)")


        banks = [ctx.enter_context(nc.psum_tensor(f"bank{i}", [P, 512], F32)) for i in range(8)]
        s_keys, t_keys, o_keys = bank_keys()

        def ring(name, part, keys):
            return Ring(part, [sem(f"{name}{i}_full") for i in range(len(part))],
                        [sem(f"{name}{i}_free") for i in range(len(part))], keys)

        S = ring("S", banks[0:4], s_keys)
        TR = ring("T", banks[4:6], t_keys)
        O = ring("O", banks[6:8], o_keys)

        DMAS = {"x0": 1, "x1": 1, "ctx": 4, "gates": 2, "l0x": 3, "wk1": 1, "l1x": 3, "l2x": 2, "l3x": 3, "mask": 1,
                "l1f": 4, "l2f": 2, "l3f": 6, **{f"expert{k}": 2 for k in range(E + 1)}}
        ld_sem = {n: sem("loaded_" + n) for n in DMAS}

        def loaded(name):
            return ld_sem[name], 16 * DMAS[name]

        const_ready = sem("const_ready")
        pool_step = sem("pool_step")
        dve_step = sem("dve_step")
        gates_ready = sem("gates_ready")
        m0_ready = sem("m0_ready")
        v2T_ready = sem("v2T_ready")
        lnS_ready = sem("lnS_ready")
        w1S_ready = sem("w1S_ready")
        w1S_high = sem("w1S_high")
        pen_ready = sem("pen_ready")
        wstat_ready = sem("wstat_ready")
        wall_ready = sem("wall_ready")
        wq_ready = sem("wq_ready")
        ln_ready = sem("ln_ready")
        xq_ready = sem("xq_ready")
        att_exp = sem("att_exp")
        att_ready = sem("att_ready")
        bmax_ready = sem("bmax_ready")
        bmax_all = sem("bmax_all")
        bat_sub = sem("bat_sub")
        bat_exp = sem("bat_exp")
        prod_ready = sem("prod_ready")
        wb0_ready = sem("wb0_ready")
        gap_ready = sem("gap_ready")
        gap_exp = sem("gap_exp")
        p_exp = sem("p_exp")
        p_recip = sem("p_recip")
        p_ready = sem("p_ready")
        pT_used = sem("pT_used")
        amax_ready = sem("amax_ready")
        amax_all = sem("amax_all")
        s1_ready = sem("s1_ready")
        hq_ready = sem("hq_ready")
        tscale_ready = sem("tscale_ready")
        gscale_ready = sem("gscale_ready")
        gq_ready = sem("gq_ready")
        gub_ready = sem("gub_ready")
        pick_ready = sem("pick_ready")
        biased = sem("biased")
        x_final = sem("x_final")
        stored = sem("stored")

        def ln_done(layer, b):
            return ln_ready, 2 * LAYERS.index(layer) + b + 1

        def lnT_done(layer, b):
            return TR.freed(("lnT", layer, b))

        def pT_read(layer, n):
            if n % TB == TB - 1:
                return O.filled((layer, n // TB))
            g = T * (layer == "L2x") + n
            return pT_used, g + 1 - g // TB

        block = ctx.enter_context(nc.Block())

        @block.sync
        def _(sp):
            def ld(name, dst, src):
                sp.dma_start(dst, src).then_inc(ld_sem[name], 16)

            xr = a["x"].rearrange("b (t p) d -> p (b t) d", p=P)
            ld("x0", x[:, 0:TB, :], xr[:, 0:TB, :])
            ld("ctx", ctxT[:, :, :], a["ctxT"])
            ld("ctx", simw[:, :], a["simw"])
            ld("x1", x[:, TB:T, :], xr[:, TB:T, :])
            ld("wk1", wkv1[:, 0, :], a["wk1"])
            ld("mask", mask[:, :, :], a["mask"].rearrange("b (t p) r -> p (b t) r", p=P))
            ld("ctx", ctx_rows[:, :, :], a["ctx_rows"])
            ld("ctx", b_sim[:, :], a["b_sim"])
            ld("l0x", wqv0[:, :, :], a["wqv0"])
            ld("l0x", bqv0[:, :], a["bqv0"].partition_broadcast(P))
            ld("l0x", w_router[:, :], a["w_router"])
            ld("l1x", wkv1[:, 1, :], a["wv1"])
            ld("l1x", wqT1[:, :, :], a["wqT1"])
            ld("l1x", wo1[:, :, :], a["wo1"])
            ld("l2x", w2x[:, :, :], a["w2x"])
            ld("l2x", bo2[:, :], a["bo2"].partition_broadcast(P))
            ld("l3x", w3x[:, :, :], a["w3x"])
            ld("l3x", b3x[:, :], a["b3x"])
            ld("l3x", row_bv3[:, :], a["bv3"])
            for k in range(E + 1):
                ld(f"expert{k}", experts[:, k, 0, :], a["w1_0"][:, k, :])
                ld(f"expert{k}", experts[:, k, 1, :], a["w2_0"][:, k, :])
            ld("l1f", fw1[:, :], a["fw1"])
            ld("l1f", fw2[:, :, :], a["fw2"])
            ld("l1f", fb1[:, :], a["fb1"])
            ld("l1f", b2_1[:, :], a["b2_1"].partition_broadcast(P))
            ld("l2f", fw_gu[:, :, :], a["fw_gu"])
            ld("l2f", fw_d[:, :, :], a["fw_d"])
            ld("l3f", wr3[:, :], a["wr3"])
            ld("l3f", br3[:, :], a["br3"])
            ld("l3f", b1_3[:, :, :], a["b1_3"])
            sp.wait_ge(*O.filled(("y0", B - 1, E)))
            ld("l3f", experts[:, 0:E, 0, :], a["w1_3"])
            ld("l3f", experts[:, 0:E, 1, :], a["w2_3"])
            sp.wait_ge(*O.filled(("L1x", B - 1)))
            ld("l3f", b2_flat, a["b2_3"])
            outr = out.rearrange("b (t p) d -> p (b t) d", p=P)
            for b in range(B):
                sp.wait_ge(x_final, b + 1)
                sp.dma_start(outr[:, b * TB:b * TB + TB, :], x[:, b * TB:b * TB + TB, :]).then_inc(stored, 16)
            sp.wait_ge(stored, 16 * B)

        @block.gpsimd
        def _(pool):
            pool.dma_start(gates[:, 0:4], a["g_xattn"].partition_broadcast(P)).then_inc(ld_sem["gates"], 16)
            pool.dma_start(gates[:, 4:8], a["g_ffn"].partition_broadcast(P)).then_inc(ld_sem["gates"], 16)
            pool.memset(ident[:, :], 0.0).then_inc(pool_step, 1)
            pool.memset(headmask[:, :], 1.0).then_inc(pool_step, 1)
            pool.memset(ones[:, :], 1.0)
            pool.memset(inv_seq[:, :], 1.0 / SEQ)
            pool.memset(magic[:, :], MAGIC)
            pool.iota(iota8[:, :], pattern=[[1, E]], base=0, channel_multiplier=0,
                      allow_small_or_imprecise_dtypes=True).then_inc(const_ready, 1)
            pool.wait_ge(pool_step, 2)
            pool.affine_select(out=ident[:, :], in_=ident[:, :], compare_op=ALU.not_equal, fill=1.0,
                               base=0, pattern=[[-1, P]], channel_multiplier=1).then_inc(const_ready, 1)
            pool.affine_select(out=headmask[:, :], in_=headmask[:, :], compare_op=ALU.is_ge, fill=0.0,
                               base=0, pattern=[[-DH2, H]], channel_multiplier=1).then_inc(pool_step, 1)
            pool.wait_ge(pool_step, 3)
            pool.affine_select(out=headmask[:, :], in_=headmask[:, :], compare_op=ALU.is_ge, fill=0.0,
                               base=DH2 - 1, pattern=[[DH2, H]], channel_multiplier=-1).then_inc(const_ready, 1)
            pool.wait_ge(const_ready, 2)
            pool.tensor_copy(identb[:, :], ident[:, :]).then_inc(const_ready, 1)
            for b in range(B):
                pool.wait_ge(bmax_ready, b + 1)
                pool.partition_all_reduce(bat[:, b, 1:2], bat[:, b, 0:1], P, RMAX).then_inc(bmax_all, 1)

            def add_bias(layer, bias, gate):
                first = (B + 1) * (layer == "L2x")
                pool.wait_ge(gates_ready, 1)
                pool.tensor_tensor(bias[:, :], bias[:, :], G[:, gate:gate + 1].to_broadcast([P, D]),
                                   ALU.mult).then_inc(biased, 1)
                pool.wait_ge(biased, first + 1)
                for b in range(B):
                    rows = x[:, b * TB:b * TB + TB, :]
                    pool.wait_ge(*ln_done(layer, b))
                    pool.tensor_tensor(rows, rows, bias[:, :].unsqueeze(1).to_broadcast([P, TB, D]),
                                       ALU.add).then_inc(biased, 1)

            def weight_totals():
                pool.wait_ge(wstat_ready, 1)
                pool.partition_all_reduce(wall[:, 0:2], wstat[:, 0:2], P, RMAX)
                pool.partition_all_reduce(wall[:, 2:5], wstat[:, 2:5], P, RADD).then_inc(wall_ready, 1)

            def normalise(layer):
                for n in range(T):
                    pool.wait_ge(p_recip, T * (layer == "L2x") + n + 1)
                    v = pr4[n % 4].rearrange("p (h r) -> p h r", h=H)
                    pool.tensor_tensor(v, v, psums[:, n % 4, 1, :].unsqueeze(2).to_broadcast([P, H, R]),
                                       ALU.mult).then_inc(p_ready, 1)

            pool.wait_ge(*loaded("l0x"))
            add_bias("L0x", bqv0, 0)
            for b in range(B):
                for k in range(E + 1):
                    n = b * (E + 1) + k
                    pool.wait_ge(*loaded(f"expert{k}"))
                    if n == 1:
                        pool.wait_ge(*TR.filled(("n1", B - 1, len(TCH) - 1)))
                    if n >= 2:
                        pool.wait_ge(*S.filled(("h0", (n - 2) // (E + 1), (n - 2) % (E + 1), C - 1)))
                    pool.tensor_copy(w1S[:, n % 2, 0, :], experts[:, k, 0, :]).then_inc(w1S_high, 1)
                    pool.wait_ge(w1S_high, n + 1)
                    pool.tensor_tensor(w1S[:, n % 2, 1, :], experts[:, k, 0, :], w1S[:, n % 2, 0, :],
                                       ALU.subtract).then_inc(w1S_ready, 1)
                    if n == 6:
                        weight_totals()
            normalise("L1x")
            for i in range(2):
                pool.wait_ge(amax_ready, i + 1)
                pool.partition_all_reduce(hall[:, i:i + 1], hmax[:, B * C + i:B * C + i + 1], P,
                                          RMAX).then_inc(amax_all, 1)
            pool.wait_ge(*loaded("l2x"))
            add_bias("L2x", bo2, 2)
            normalise("L2x")

        @block.scalar
        def _(act):
            def copy_out(ring_, key, dst, src):
                act.wait_ge(*ring_.filled(key))
                act.activation(dst, src, ACT.Copy).then_inc(ring_.free(key), 1)

            def copy_chunks(key, dst, c0, c1):
                bank = TR.bank(key)
                act.wait_ge(*TR.filled(key))
                full = min(c1, HR // P)
                ins = act.activation(dst[:, c0:full, :],
                                     bank[:, 0:(full - c0) * P].rearrange("p (c k) -> p c k", k=P), ACT.Copy)
                if full < c1:
                    ins = act.activation(dst[0:HR - full * P, full, :],
                                         bank[0:HR - full * P, (full - c0) * P:(full - c0 + 1) * P], ACT.Copy)
                ins.then_inc(TR.free(key), 1)

            def transposed(layer, b):
                copy_out(TR, ("lnT", layer, b), lnTf[:, b * SEQ:b * SEQ + SEQ], TR.bank(("lnT", layer, b))[:, :])

            def quantised(layer, b):
                copy_out(TR, ("xqT", layer, b), xqT[:, b * SEQ:b * SEQ + SEQ],
                         TR.bank(("xqT", layer, b))[:, :].bitcast(BF16)[:, 0:SEQ])

            act.wait_ge(*loaded("gates"))
            act.activation(G[:, :], gates[:, :], ACT.Tanh).then_inc(gates_ready, 1)
            def keys_values_1(w):
                for i in range(3):
                    n = min(3, NK1 - 3 * i)
                    copy_out(S, ("kv1", w, i), kv1T[:, w, 3 * i:3 * i + n, :],
                             S.bank(("kv1", w, i))[:, 0:n * B * R].rearrange("p (c r) -> p c r", c=n))

            transposed("L0x", 0)
            keys_values_1(0)
            transposed("L0x", 1)
            for b in range(B):
                act.wait_ge(*S.freed(("sim", b)))
                act.activation(att[:, b, :, :], att[:, b, :, :], ACT.Exp).then_inc(att_exp, 1)
                act.wait_ge(bat_sub, b + 1)
                act.activation(bat[:, b, 8:12], bat[:, b, 8:12], ACT.Exp,
                               accum_out=bat[:, b, 2:3]).then_inc(bat_exp, 1)
            keys_values_1(1)

            def copy_heads(name, dst):
                for i, (h0, h1) in enumerate(HALVES):
                    copy_out(S, (name, i), dst[:, :, h0 * R:h1 * R].rearrange("p b (h r) -> p h b r", r=R),
                             S.bank((name, i))[:, 0:(h1 - h0) * B * R].rearrange("p (h b r) -> p h b r", b=B, r=R))

            copy_heads("m1", m1)
            for b in range(B):
                copy_out(TR, ("aT0", b), attT[:, b, :], TR.bank(("aT0", b))[0:R, :])
            for b in range(B):
                copy_out(S, ("hq", b), hqT[:, b, :], S.bank(("hq", b))[:, :])

            copy_heads("n1T", nT)
            copy_out(S, "kv2", kv2T[:, :, :], S.bank("kv2")[:, 0:2 * B * R].rearrange("p (w r) -> p w r", w=2))
            act.wait_ge(*loaded("l3x"))
            act.wait_ge(*S.filled("k3"))
            act.activation(k3T[:, :], S.bank("k3")[:, 0:B * R], ACT.Identity, bias=b3x[:, 1:2]).then_inc(S.free("k3"), 1)
            for b in range(B):
                for i, (c0, c1) in enumerate(TCH):
                    copy_chunks(("n1", b, i), n1[:, b, :, :], c0, c1)
                if b == 0:
                    act.wait_ge(*S.filled("m3"))
                    act.activation(cb3[:, :], S.bank("m3")[0:1, B * R:2 * B * R], ACT.Copy)
                    act.activation(m3[:, :], S.bank("m3")[:, 0:B * R], ACT.Copy).then_inc(S.free("m3"), 1)
                    copy_out(S, "v3", v3[:, :, :], S.bank("v3")[0:R, 0:B * D].rearrange("r (b d) -> r b d", b=B))
            for b in range(B):
                transposed("L0f", b)
            for b in range(B):
                act.wait_ge(gap_ready, b + 1)
                act.activation(tw[:, b, 1, :], tw[:, b, 0, :], ACT.Exp).then_inc(gap_exp, 1)
            for b in range(B):
                for k in range(E + 1):
                    n = b * (E + 1) + k
                    for c in range(C):
                        key = ("h0", b, k, c)
                        act.wait_ge(*S.filled(key))
                        if n >= 2 and c == 0:
                            act.wait_ge(*O.filled(("y0", (n - 2) // (E + 1), (n - 2) % (E + 1))))
                        act.activation(hT[:, n % 2, c, :], S.bank(key)[:, :], ACT.Silu).then_inc(S.free(key), 1)
                    if b == 0 and k == 7:
                        for bb in range(B):
                            for j, (c0, c1) in enumerate(TCH):
                                copy_chunks(("v2", bb, j), v2[:, bb, :, :], c0, c1)

                    if b == B - 1 and k == 4:
                        transposed("L1x", 0)

            def attention(layer, scale):
                base = T * (layer == "L2x")

                def exps(n):
                    act.wait_ge(*S.freed((layer, n, len(HEADS) - 1)))
                    act.activation(pr4[n % 4], pr4[n % 4], ACT.Exp, scale=scale).then_inc(p_exp, 1)

                if layer == "L2x":
                    for b in range(B):
                        transposed("L2x", b)
                        copy_out(S, ("q2", b), q2T[:, b, :], S.bank(("q2", b))[:, :])
                exps(0)
                for n in range(T):
                    if n >= 2:
                        act.wait_ge(*pT_read(layer, n - 2))
                    for i, (c0, c1) in enumerate(TCH):
                        if i == len(TCH) - 1 and n == 0:
                            exps(1)
                        if i == len(TCH) - 1 and n + 2 < T:
                            exps(n + 2)
                        copy_chunks(("pT", layer, n, i), prT[:, n % 2, :, :], c0, c1)
                    if layer == "L2x" and n == TB:
                        copy_out(O, ("L2x", 0), o2T[:, 0, :], O.bank(("L2x", 0))[:, :])
                if layer == "L2x":
                    copy_out(O, ("L2x", 1), o2T[:, 1, :], O.bank(("L2x", 1))[:, :])

            transposed("L1x", 1)
            attention("L1x", DH1 ** -0.5)
            for b in range(B):
                quantised("L1f", b)
            act.wait_ge(s1_ready, 1)
            for b in range(B):
                for c in range(C):
                    key = ("h1", b, c)
                    act.wait_ge(*S.filled(key))
                    act.activation(hT[:, b, c, :], S.bank(key)[:, :], ACT.Gelu, bias=wsc[:, 4 + c:5 + c],
                                   scale=wsc[:, 2:3]).then_inc(S.free(key), 1)
            attention("L2x", DH2 ** -0.5)
            quantised("L2f", 0)
            for n in range(T + 2):
                if n < T:
                    act.wait_ge(tscale_ready, n // TB + 1)
                    if n >= 2:
                        act.wait_ge(*S.freed(("up", n - 2)))
                    act.wait_ge(*S.filled(("gate", n)))
                    act.activation(silu[:, n % 2, :], S.bank(("gate", n))[:, :], ACT.Silu,
                                   scale=tsc[:, 2, n:n + 1]).then_inc(S.free(("gate", n)), 1)
                if n == 1:
                    quantised("L2f", 1)
                if 1 <= n <= T:
                    m = n - 1
                    act.wait_ge(gscale_ready, m + 1)
                    act.activation(guf[:, m % 2, :], guf[:, m % 2, :], ACT.Identity, bias=magic[:, :],
                                   scale=tsc[:, 5, m:m + 1]).then_inc(gq_ready, 1)
                if n >= 2:
                    m = n - 2
                    copy_out(TR, ("guT", m), guT[:, m, :, :],
                             TR.bank(("guT", m))[:, :].bitcast(BF16)[:, 0:FF].rearrange("p (c k) -> p c k", c=C))
            for b in range(B):
                transposed("L3x", b)
            for b in range(B):
                act.wait_ge(*S.freed(("s3", b)))
                act.activation(att[:, b, :, :], att[:, b, :, :], ACT.Exp, scale=D ** -0.5).then_inc(att_exp, 1)
            for b in range(B):
                copy_out(TR, ("aT3", b), attT[:, b, :], TR.bank(("aT3", b))[0:R, :])
            for b in range(B):
                transposed("L3f", b)
            for b in range(B):
                act.wait_ge(pick_ready, b + 1)
                for c in range(C):
                    key = ("h3", b, c)
                    act.wait_ge(*S.filled(key))
                    act.activation(hT[:, b, c, :], S.bank(key)[:, :], ACT.Relu,
                                   bias=b1s[:, b, c:c + 1]).then_inc(S.free(key), 1)

        @block.tensor
        def _(pe):
            def acquire(ring_, key):
                if ring_.reused(key):
                    pe.wait_ge(*ring_.freed_before(key))
                return ring_.bank(key)

            def transpose_rows(layer, b):
                key = ("lnT", layer, b)
                bank = acquire(TR, key)
                pe.wait_ge(*ln_done(layer, b))
                for t in range(TB):
                    ins = pe.transpose(bank[:, t * P:t * P + P], ln[:, b * TB + t, :], ident[:, :])
                ins.then_inc(TR.full(key), 1)

            def transpose_quantised(layer, b):
                key = ("xqT", layer, b)
                bank = acquire(TR, key)[:, :].bitcast(BF16)
                pe.wait_ge(xq_ready, B * (layer == "L2f") + b + 1)
                for t in range(TB):
                    ins = pe.transpose(bank[:, t * P:t * P + P], xqb[:, b * TB + t, :], identb[:, :])
                ins.then_inc(TR.full(key), 1)

            def transpose_chunks(key, src, c0, c1, id_):
                bank = acquire(TR, key)
                for c in range(c0, c1):
                    n = min(P, HR - c * P)
                    ins = pe.transpose(bank[0:n, (c - c0) * P:(c - c0 + 1) * P], src[:, c * P:c * P + n], id_[:, :])
                ins.then_inc(TR.full(key), 1)

            pe.wait_ge(*loaded("ctx"))
            bank = acquire(S, "cb0")
            pe.matmul(bank[0:1, 0:B * R], simw[:, 1:2], ctxTf, start=True, stop=True).then_inc(S.full("cb0"), 1)
            pe.wait_ge(const_ready, 4)
            def keys_values_1(w):
                for i in range(3):
                    bank = acquire(S, ("kv1", w, i))
                    for c in range(3 * i, min(3 * i + 3, NK1)):
                        ins = pe.matmul(bank[:, (c - 3 * i) * B * R:(c - 3 * i + 1) * B * R],
                                        wkv1[:, w, c * P:c * P + P], ctxTf, start=True, stop=True)
                    ins.then_inc(S.full(("kv1", w, i)), 1)

            transpose_rows("L0x", 0)
            pe.wait_ge(*loaded("wk1"))
            keys_values_1(0)
            transpose_rows("L0x", 1)
            pe.wait_ge(m0_ready, 1)
            pe.wait_ge(*S.freed("cb0"))
            for b in range(B):
                bank = acquire(S, ("sim", b))
                pe.wait_ge(*lnT_done("L0x", b))
                for t in range(TB):
                    o = bank[:, t * R:t * R + R]
                    pe.matmul(o, lnT[:, b * TB + t, :], m0[:, b, :], start=True, stop=False)
                    ins = pe.matmul(o, ones[0:1, :], cb0[:, b * R:b * R + R], start=False, stop=True)
                ins.then_inc(S.full(("sim", b)), 1)
            pe.wait_ge(*loaded("l1x"))
            keys_values_1(1)

            def per_head(name, w, weight):
                for i, (h0, h1) in enumerate(HALVES):
                    key = (name, i)
                    bank = acquire(S, key)
                    pe.wait_ge(*S.freed(("kv1", w, 2)))
                    for h in range(h0, h1):
                        p0, c = DH1 * (h // NK1), h % NK1
                        ins = pe.matmul(bank[:, (h - h0) * B * R:(h - h0 + 1) * B * R], weight[p0:p0 + DH1, c, :],
                                        kv1T[p0:p0 + DH1, w, c, :], start=True, stop=True)
                    ins.then_inc(S.full(key), 1)

            per_head("m1", 0, wqT1)
            for b in range(B):
                bank = acquire(S, ("hc", b))
                pe.wait_ge(bat_exp, b + 1)
                pe.matmul(bank[:, 0:1], ones[:, :], bat[:, b, 2:3], start=True, stop=True)
                for t in range(TB):
                    ins = pe.matmul(bank[:, 1:2], ln[:, b * TB + t, :], bat[:, b, 8 + t:9 + t],
                                    start=(t == 0), stop=(t == TB - 1))
                ins.then_inc(S.full(("hc", b)), 1)
            for b in range(B):
                bank = acquire(TR, ("aT0", b))
                pe.wait_ge(att_ready, b + 1)
                for t in range(TB):
                    ins = pe.transpose(bank[0:R, t * P:t * P + P], att[:, b, t, :], ident[:, :])
                ins.then_inc(TR.full(("aT0", b)), 1)
            for b in range(B):
                bank = acquire(S, ("hq", b))
                pe.wait_ge(*TR.freed(("aT0", b)))
                pe.matmul(bank[:, :], ctx_rows[:, b, :], attT[:, b, :], start=True, stop=True).then_inc(S.full(("hq", b)), 1)
            pe.wait_ge(*loaded("l0x"))
            for b in range(B):
                bank = acquire(O, ("L0x", b))
                pe.wait_ge(wb0_ready, b + 1)
                pe.wait_ge(*S.freed(("hq", b)))
                pe.wait_ge(prod_ready, b + 1)
                for t in range(TB):
                    o = bank[:, t * D:t * D + D]
                    pe.matmul(o, lnT[:, b * TB + t, :], wb0[:, b, :], start=True, stop=False)
                    pe.matmul(o, hqT[:, b, t * P:t * P + P], wqv0[:, 1, :], start=False, stop=False)
                    ins = pe.matmul(o, prodT[:, b, t * P:t * P + P], wqv0[:, 2, :], start=False, stop=True)
                ins.then_inc(O.full(("L0x", b)), 1)

            def m3_and_v3():
                bank = acquire(S, "m3")
                pe.wait_ge(*S.freed("k3"))
                pe.matmul(bank[:, 0:B * R], w3x[:, 0, :], k3T[:, :], start=True, stop=True)
                pe.matmul(bank[0:1, B * R:2 * B * R], b3x[:, 0:1], k3T[:, :], start=True, stop=True).then_inc(S.full("m3"), 1)
                bank = acquire(S, "v3")
                for b in range(B):
                    pe.matmul(bank[0:R, b * D:b * D + D], ctxT[:, b, :], w3x[:, 2, :], start=True, stop=False)
                    ins = pe.matmul(bank[0:R, b * D:b * D + D], ones[0:1, 0:R], row_bv3[:, :], start=False, stop=True)
                ins.then_inc(S.full("v3"), 1)

            per_head("n1T", 1, wo1)
            pe.wait_ge(*loaded("l2x"))
            bank = acquire(S, "kv2")
            pe.matmul(bank[:, 0:B * R], w2x[:, 1, :], ctxTf, start=True, stop=True)
            pe.matmul(bank[:, B * R:2 * B * R], w2x[:, 2, :], ctxTf, start=True, stop=True).then_inc(S.full("kv2"), 1)
            pe.wait_ge(*loaded("l3x"))
            bank = acquire(S, "k3")
            pe.matmul(bank[:, 0:B * R], w3x[:, 1, :], ctxTf, start=True, stop=True).then_inc(S.full("k3"), 1)
            pe.wait_ge(*S.freed(("n1T", len(HALVES) - 1)))
            for b in range(B):
                for i, (c0, c1) in enumerate(TCH):
                    transpose_chunks(("n1", b, i), nT[:, b, :], c0, c1, ident)
                if b == 0:
                    m3_and_v3()
            for b in range(B):
                transpose_rows("L0f", b)
            for b in range(B):
                bank = acquire(S, ("router", b))
                pe.wait_ge(*lnT_done("L0f", b))
                for t in range(TB):
                    ins = pe.matmul(bank[:, t * E:t * E + E], lnT[:, b * TB + t, :], w_router[:, :], start=True, stop=True)
                ins.then_inc(S.full(("router", b)), 1)

            def expert_up(b, k):
                n = b * (E + 1) + k
                pe.wait_ge(lnS_ready, b + 1)
                pe.wait_ge(w1S_ready, n + 1)
                for c in range(C):
                    bank = acquire(S, ("h0", b, k, c))
                    for i, (w, r) in enumerate(((0, 0), (0, 1), (1, 0))):
                        ins = pe.matmul(bank[:, :], w1S[:, n % 2, w, c * P:c * P + P], lnS[:, r, b * SEQ:b * SEQ + SEQ],
                                        start=(i == 0), stop=(i == 2))
                    ins.then_inc(S.full(("h0", b, k, c)), 1)

            def expert_down(b, k):
                bank = acquire(O, ("y0", b, k))
                pe.wait_ge(*S.freed(("h0", b, k, C - 1)))
                for t in range(TB):
                    for c in range(C):
                        ins = pe.matmul(bank[:, t * D:t * D + D], hT[:, (b * (E + 1) + k) % 2, c, t * P:t * P + P],
                                        experts[:, k, 1, c * P:c * P + P], start=(c == 0), stop=(c == C - 1))
                ins.then_inc(O.full(("y0", b, k)), 1)

            order = [(b, k) for b in range(B) for k in range(E + 1)]
            for i, (b, k) in enumerate(order):
                if b == 0:
                    pe.wait_ge(*loaded(f"expert{k}"))
                expert_up(b, k)
                if i >= 1:
                    expert_down(*order[i - 1])
                if b == 0 and k == 7:
                    for bb in range(B):
                        pe.wait_ge(v2T_ready, bb + 1)
                        for j, (c0, c1) in enumerate(TCH):
                            transpose_chunks(("v2", bb, j), v2T[bb], c0, c1, ident)

                if b == B - 1 and k == 4:
                    transpose_rows("L1x", 0)
            expert_down(*order[-1])

            def attention(layer):
                def scores(n):
                    for i, (h0, h1) in enumerate(HEADS):
                        key = (layer, n, i)
                        bank = acquire(S, key)
                        o = bank[:, 0:(h1 - h0) * R]
                        if layer == "L1x":
                            ins = pe.matmul(o, lnT[:, n, :], m1[:, n // TB, h0 * R:h1 * R], start=True, stop=True)
                        else:
                            pe.matmul(o, q2T[:, n // TB, n % TB * P:(n % TB + 1) * P],
                                      k2blk[:, n // TB, h0:h1, :], start=True, stop=False)
                            ins = pe.matmul(o.rearrange("p (h r) -> p h r", h=h1 - h0), identb[:, :],
                                            penalty[:, n, :].unsqueeze(1).to_broadcast([P, h1 - h0, R]),
                                            start=False, stop=True)
                        ins.then_inc(S.full(key), 1)

                def weighted(n):
                    key = (layer, n // TB)
                    bank = acquire(O, key) if n % TB == 0 else O.bank(key)
                    o = bank[:, n % TB * P:(n % TB + 1) * P]
                    pe.wait_ge(*TR.freed(("pT", layer, n, len(TCH) - 1)))
                    for c in range(CH):
                        k = min(P, HR - c * P)
                        w, v = prT[0:k, n % 2, c, :], (n1 if layer == "L1x" else v2)[0:k, n // TB, c, :]
                        l, r = (w, v) if layer == "L1x" else (v, w)
                        ins = pe.matmul(o, l, r, start=(c == 0), stop=(c == CH - 1))
                    ins.then_inc(O.full(key) if n % TB == TB - 1 else pT_used, 1)

                def project(b):
                    bank = acquire(O, ("o2", b))
                    pe.wait_ge(*O.freed(("L2x", b)))
                    for t in range(TB):
                        o = bank[:, t * D:t * D + D]
                        ins = pe.matmul(o, o2T[:, b, t * P:t * P + P], w2x[:, 3, :], start=True, stop=True)
                    ins.then_inc(O.full(("o2", b)), 1)

                def queries(b):
                    bank = acquire(S, ("q2", b))
                    pe.wait_ge(*lnT_done("L2x", b))
                    pe.matmul(bank[:, :], w2x[:, 0, :], lnTf[:, b * SEQ:b * SEQ + SEQ],
                              start=True, stop=True).then_inc(S.full(("q2", b)), 1)

                if layer == "L2x":
                    transpose_rows("L2x", 0)
                    queries(0)
                    pe.wait_ge(pen_ready, 1)
                    pe.wait_ge(*S.freed(("q2", 0)))
                else:
                    pe.wait_ge(*lnT_done("L1x", 0))
                scores(0)
                transpose_rows(layer, 1)
                if layer == "L2x":
                    queries(1)
                    pe.wait_ge(*S.freed(("q2", 1)))
                else:
                    pe.wait_ge(*lnT_done("L1x", 1))
                scores(1)
                scores(2)
                for n in range(T):
                    pe.wait_ge(p_ready, T * (layer == "L2x") + n + 1)
                    for i, (c0, c1) in enumerate(TCH):
                        if i == len(TCH) - 1:
                            if n + 3 < T:
                                scores(n + 3)
                            else:
                                weighted(n - 1)
                        transpose_chunks(("pT", layer, n, i), pr4[n % 4], c0, c1, ident)
                    if layer == "L2x" and n == TB + 1:
                        project(0)
                    if 1 <= n and n + 3 < T:
                        weighted(n - 1)
                weighted(T - 1)
                if layer == "L2x":
                    project(1)

            attention("L1x")
            for b in range(B):
                transpose_quantised("L1f", b)
            pe.wait_ge(wq_ready, 1)
            for b in range(B):
                pe.wait_ge(*TR.freed(("xqT", "L1f", b)))
                for c in range(C):
                    bank = acquire(S, ("h1", b, c))
                    pe.matmul(bank[:, :], fw1q[:, c * P:c * P + P], xqT[:, b * SEQ:b * SEQ + SEQ],
                              start=True, stop=True).then_inc(S.full(("h1", b, c)), 1)
            for b in range(B):
                bank = acquire(O, ("L1f", b))
                pe.wait_ge(hq_ready, b + 1)
                for t in range(TB):
                    n = b * TB + t
                    for c in range(C):
                        ins = pe.matmul(bank[:, t * D:t * D + D], hqb[:, c, n * P:n * P + P], fw2q[:, c, :],
                                        start=(c == 0), stop=(c == C - 1))
                ins.then_inc(O.full(("L1f", b)), 1)
            attention("L2x")
            transpose_quantised("L2f", 0)
            for n in range(T + 3):
                if n == 2:
                    transpose_quantised("L2f", 1)
                if n < T:
                    if n % TB == 0:
                        pe.wait_ge(*TR.freed(("xqT", "L2f", n // TB)))
                    for w, name in enumerate(("gate", "up")):
                        bank = acquire(S, (name, n))
                        pe.matmul(bank[:, :], xqT[:, n * P:n * P + P], guq[:, w, :],
                                  start=True, stop=True).then_inc(S.full((name, n)), 1)
                if 2 <= n <= T + 1:
                    m = n - 2
                    bank = acquire(TR, ("guT", m))[:, :].bitcast(BF16)
                    pe.wait_ge(gub_ready, m + 1)
                    for c in range(C):
                        ins = pe.transpose(bank[:, c * P:c * P + P], gub[:, m % 2, c * P:c * P + P], identb[:, :])
                    ins.then_inc(TR.full(("guT", m)), 1)
                if n >= 3:
                    m = n - 3
                    key = ("L2f", m // TB)
                    bank = acquire(O, key) if m % TB == 0 else O.bank(key)
                    pe.wait_ge(*TR.freed(("guT", m)))
                    for c in range(C):
                        ins = pe.matmul(bank[:, m % TB * D:(m % TB + 1) * D], guT[:, m, c, :], dq[:, c, :],
                                        start=(c == 0), stop=(c == C - 1))
                    if m % TB == TB - 1:
                        ins.then_inc(O.full(key), 1)
            for b in range(B):
                transpose_rows("L3x", b)
            for b in range(B):
                bank = acquire(S, ("s3", b))
                pe.wait_ge(*lnT_done("L3x", b))
                for t in range(TB):
                    o = bank[:, t * R:t * R + R]
                    pe.matmul(o, lnT[:, b * TB + t, :], m3[:, b * R:b * R + R], start=True, stop=False)
                    ins = pe.matmul(o, ones[0:1, :], cb3[:, b * R:b * R + R], start=False, stop=True)
                ins.then_inc(S.full(("s3", b)), 1)
            for b in range(B):
                bank = acquire(TR, ("aT3", b))
                pe.wait_ge(att_ready, B + b + 1)
                for t in range(TB):
                    ins = pe.transpose(bank[0:R, t * P:t * P + P], att[:, b, t, :], ident[:, :])
                ins.then_inc(TR.full(("aT3", b)), 1)
            for b in range(B):
                bank = acquire(O, ("L3x", b))
                pe.wait_ge(*TR.freed(("aT3", b)))
                for t in range(TB):
                    ins = pe.matmul(bank[:, t * D:t * D + D], attT[:, b, t * P:t * P + P], v3[:, b, :],
                                    start=True, stop=True)
                ins.then_inc(O.full(("L3x", b)), 1)
            for b in range(B):
                transpose_rows("L3f", b)
            pe.wait_ge(*loaded("l3f"))
            for b in range(B):
                bank = acquire(S, ("mean", b))
                for t in range(TB):
                    ins = pe.matmul(bank[:, 0:1], ln[:, b * TB + t, :], inv_seq[:, :],
                                    start=(t == 0), stop=(t == TB - 1))
                ins.then_inc(S.full(("mean", b)), 1)
            for b in range(B):
                bank = acquire(S, ("pick", b))
                pe.wait_ge(*S.freed(("mean", b)))
                pe.matmul(bank[0:1, 0:E], mean3[:, b:b + 1], wr3[:, :], start=True, stop=True).then_inc(S.full(("pick", b)), 1)
            for b in range(B):
                pe.wait_ge(pick_ready, b + 1)
                for c in range(C):
                    bank = acquire(S, ("h3", b, c))
                    pe.wait_ge(*lnT_done("L3f", b))
                    pe.matmul(bank[:, :], w1s[:, b, c * P:c * P + P], lnTf[:, b * SEQ:b * SEQ + SEQ],
                              start=True, stop=True).then_inc(S.full(("h3", b, c)), 1)
            for b in range(B):
                bank = acquire(O, ("L3f", b))
                pe.wait_ge(*S.freed(("h3", b, C - 1)))
                for t in range(TB):
                    o = bank[:, t * D:t * D + D]
                    for c in range(C):
                        pe.matmul(o, hT[:, b, c, t * P:t * P + P], w2s[:, b, c * P:c * P + P],
                                  start=(c == 0), stop=False)
                    ins = pe.matmul(o, ones[0:1, :], b2s[:, b, :], start=False, stop=True)
                ins.then_inc(O.full(("L3f", b)), 1)

        @block.vector
        def _(dve):
            steps = [0]

            def step(ins):
                steps[0] += 1
                ins.then_inc(dve_step, 1)
                dve.wait_ge(dve_step, steps[0])

            def normalise(layer, b, ready=True):
                for t in range(b * TB, b * TB + TB):
                    ins = dve.bn_stats(bn[:, t, :], x[:, t, :])
                step(ins)
                for t in range(b * TB, b * TB + TB):
                    ins = dve.bn_aggr(mv[:, t, :], bn[:, t, :])
                step(ins)
                y, sq = rstd[:, b * TB:b * TB + TB], newton[:, b, 2, :]
                dve.tensor_scalar(newton[:, b, 1, :], mv[:, b * TB:b * TB + TB, 1], EPS, -0.5, ALU.add, ALU.mult)
                step(dve.tensor_scalar(newton[:, b, 0, :], mv[:, b * TB:b * TB + TB, 1], EPS, 0.5, ALU.add, ALU.mult))
                step(dve.tensor_scalar(y.bitcast(I32), newton[:, b, 0, :].bitcast(I32), -0.5, GUESS, ALU.mult, ALU.add))
                for _ in range(3):
                    step(dve.tensor_tensor(sq, y, y, ALU.mult))
                    step(dve.tensor_tensor(sq, sq, newton[:, b, 1, :], ALU.mult))
                    step(dve.scalar_tensor_tensor(y, sq, 1.5, y, ALU.add, ALU.mult))
                for t in range(b * TB, b * TB + TB):
                    ins = dve.tensor_scalar(ln[:, t, :], x[:, t, :], mv[:, t, 0:1], rstd[:, t:t + 1],
                                            ALU.subtract, ALU.mult)
                ins.then_inc(ln_ready, 1)

            def update(key, b, gate, src=None):
                rows = x[:, b * TB:b * TB + TB, :]
                dve.wait_ge(*O.filled(key))
                dve.scalar_tensor_tensor(rows, O.bank(key)[:, :].rearrange("p (t d) -> p t d", t=TB),
                                         G[:, gate:gate + 1], rows, ALU.mult, ALU.add).then_inc(O.free(key), 1)
                dve.wait_ge(*O.freed(key))

            def bc(v, n):
                return v.unsqueeze(2).to_broadcast([P, v.shape[1], n])

            dve.wait_ge(*loaded("x0"))
            normalise("L0x", 0)
            dve.wait_ge(*loaded("ctx"))
            dve.tensor_scalar(m0[:, :, :], ctxT[:, :, :], simw[:, 2:3], simw[:, 0:1], ALU.mult, ALU.add).then_inc(m0_ready, 1)
            dve.wait_ge(*S.filled("cb0"))
            dve.tensor_scalar(cb0[:, :], S.bank("cb0")[0:1, 0:B * R], b_sim[:, 0:1], None, ALU.add).then_inc(S.free("cb0"), 1)
            dve.wait_ge(*S.freed("cb0"))
            dve.wait_ge(*loaded("x1"))
            normalise("L0x", 1)
            dve.wait_ge(*loaded("mask"))
            dve.tensor_scalar(penalty[:, :, :], mask[:, :, :], 0.0, MASKED, ALU.is_equal, ALU.mult).then_inc(pen_ready, 1)
            def head_blocks():
                dve.wait_ge(*S.freed("kv2"))
                dve.wait_ge(const_ready, 4)
                for b in range(B):
                    m = headmask[:, :].unsqueeze(2).to_broadcast([P, H, R])

                    def blocks(w):
                        return kv2T[:, w, b * R:b * R + R].unsqueeze(1).to_broadcast([P, H, R])
                    dve.tensor_tensor(k2blk[:, b, :, :], blocks(0), m, ALU.mult)
                    dve.tensor_tensor(v2T[b].rearrange("p (h r) -> p h r", h=H), blocks(1), m,
                                      ALU.mult).then_inc(v2T_ready, 1)

            def softmax_in(bank_key, b):
                v = S.bank(bank_key)[:, 0:TB * R].rearrange("p (t r) -> p t r", t=TB)
                dve.wait_ge(*S.filled(bank_key))
                step(dve.tensor_reduce(amax[:, b, :], v, AX, ALU.max))
                dve.tensor_tensor(att[:, b, :, :], v, bc(amax[:, b, :], R), ALU.subtract).then_inc(S.free(bank_key), 1)

            def softmax_out(b, count):
                dve.wait_ge(att_exp, count)
                step(dve.tensor_reduce(asum[:, b, :], att[:, b, :, :], AX, ALU.add))
                step(dve.reciprocal(asum[:, b, :], asum[:, b, :]))
                dve.tensor_tensor(att[:, b, :, :], att[:, b, :, :], bc(asum[:, b, :], R), ALU.mult).then_inc(att_ready, 1)

            for b in range(B):
                softmax_in(("sim", b), b)
                dve.tensor_reduce(bat[:, b, 0:1], amax[:, b, :], AX, ALU.max).then_inc(bmax_ready, 1)
            for b in range(B):
                dve.wait_ge(bmax_all, b + 1)
                dve.tensor_scalar(bat[:, b, 8:12], amax[:, b, :], bat[:, b, 1:2], None, ALU.subtract).then_inc(bat_sub, 1)
            for b in range(B):
                softmax_out(b, b + 1)
            dve.wait_ge(*loaded("l0x"))
            for b in range(B):
                dve.wait_ge(*S.filled(("hc", b)))
                step(dve.reciprocal(bat[:, b, 3:4], S.bank(("hc", b))[:, 0:1]))
                dve.tensor_scalar(bat[:, b, 4:5], S.bank(("hc", b))[:, 1:2], bat[:, b, 3:4], None,
                                  ALU.mult).then_inc(S.free(("hc", b)), 1)
                dve.wait_ge(*S.freed(("hc", b)))
                dve.scalar_tensor_tensor(wb0[:, b, :], wqv0[:, 3, :], bat[:, b, 4:5], wqv0[:, 0, :], ALU.mult,
                                         ALU.add).then_inc(wb0_ready, 1)
            for b in range(B):
                dve.wait_ge(*S.freed(("hq", b)))
                dve.tensor_tensor(prodT[:, b, :], hqT[:, b, :], lnTf[:, b * SEQ:b * SEQ + SEQ],
                                  ALU.mult).then_inc(prod_ready, 1)
            dve.wait_ge(gates_ready, 1)
            for b in range(B):
                dve.wait_ge(biased, b + 2)
                update(("L0x", b), b, 0)
                normalise("L0f", b)

            dve.wait_ge(*TR.filled(("n1", B - 1, len(TCH) - 1)))
            for b in range(B):
                rows = slice(b * SEQ, b * SEQ + SEQ)
                dve.wait_ge(*lnT_done("L0f", b))
                step(dve.tensor_copy(lnS[:, 0, rows], lnTf[:, rows]))
                dve.tensor_tensor(lnS[:, 1, rows], lnTf[:, rows], lnS[:, 0, rows], ALU.subtract).then_inc(lnS_ready, 1)
            dve.wait_ge(const_ready, 4)
            for b in range(B):
                key = ("router", b)
                dve.wait_ge(*S.filled(key))
                dve.tensor_copy(logits[:, b, :, :], S.bank(key)[:, 0:TB * E].rearrange("p (t e) -> p t e", t=TB)).then_inc(S.free(key), 1)
                dve.wait_ge(*S.freed(key))
                for t in range(TB):
                    ins = dve.max(top[:, b, t, :], logits[:, b, t, :])
                step(ins)
                for t in range(TB):
                    dve.max_index(topi[:, b, t, :], top[:, b, t, :], logits[:, b, t, :])
                dve.tensor_tensor(tw[:, b, 0, :], top[:, b, :, 1], top[:, b, :, 0], ALU.subtract).then_inc(gap_ready, 1)
            for b in range(B):
                step(dve.tensor_copy(topf[:, b, :, :], topi[:, b, :, :]))
                dve.wait_ge(gap_exp, b + 1)
                step(dve.tensor_scalar(tw[:, b, 2, :], tw[:, b, 1, :], 1.0, None, ALU.add))
                step(dve.reciprocal(tw[:, b, 2, :], tw[:, b, 2, :]))
                step(dve.tensor_tensor(tw[:, b, 3, :], tw[:, b, 1, :], tw[:, b, 2, :], ALU.mult))
                for t in range(TB):
                    dve.tensor_scalar(cw[:, b, t, :], iota8[:, :], topf[:, b, t, 0:1], tw[:, b, 2, t:t + 1],
                                      ALU.is_equal, ALU.mult)
                    ins = dve.tensor_scalar(cw2[:, b, t, :], iota8[:, :], topf[:, b, t, 1:2], tw[:, b, 3, t:t + 1],
                                            ALU.is_equal, ALU.mult)
                step(ins)
                step(dve.tensor_tensor(cw[:, b, :, :], cw[:, b, :, :], cw2[:, b, :, :], ALU.add))

            def weight_stats():
                dve.wait_ge(*loaded("l1f"))
                dve.wait_ge(*loaded("l2f"))
                for i, (w, op) in enumerate(((fw1[:, :], ALU.max), (flat(fw2), ALU.max), (fw_gu[:, 0, :], ALU.add),
                                             (fw_gu[:, 1, :], ALU.add), (flat(fw_d), ALU.add))):
                    ins = dve.tensor_reduce(wstat[:, i:i + 1], w, AX, op, apply_absolute_value=True)
                ins.then_inc(wstat_ready, 1)

            def weight_quantise():
                dve.wait_ge(wall_ready, 1)
                step(dve.tensor_scalar(wsc[:, 0:2], wall[:, 0:2], 1e-6, 1.0 / QP, ALU.max, ALU.mult))
                step(dve.reciprocal(wsc[:, 12:14], wsc[:, 0:2]))
                step(dve.tensor_scalar(wsc[:, 14:17], wall[:, 2:5], 1.0 / (D * FF), 1e-5, ALU.mult, ALU.max))
                step(dve.reciprocal(wsc[:, 17:20], wsc[:, 14:17]))
                for i, w in enumerate((fw1[:, :], flat(fw2))):
                    ins = dve.tensor_scalar(w, w, wsc[:, 12 + i:13 + i], MAGIC, ALU.mult, ALU.add)
                ws = (fw_gu[:, 0, :], fw_gu[:, 1, :], flat(fw_d))
                for i, w in enumerate(ws):
                    ins = dve.tensor_scalar(w, w, wsc[:, 17 + i:18 + i], 1.0, ALU.mult, ALU.min)
                step(ins)
                for w in ws:
                    ins = dve.tensor_scalar(w, w, -1.0, MAGIC, ALU.max, ALU.add)
                step(ins)
                for w, q in ((fw1[:, :], fw1q[:, :]), (flat(fw2), flat(fw2q)), (fw_gu[:, 0, :], guq[:, 0, :]),
                             (fw_gu[:, 1, :], guq[:, 1, :]), (flat(fw_d), flat(dq))):
                    ins = dve.tensor_scalar(q, w, MAGIC, None, ALU.subtract)
                ins.then_inc(wq_ready, 1)

            for b in range(B):
                for k in range(E + 1):
                    key = ("y0", b, k)
                    dve.wait_ge(*O.filled(key))
                    y = O.bank(key)[:, :].rearrange("p (t d) -> p t d", t=TB)
                    if k == 0:
                        dve.tensor_copy(acc[:, b, :, :], y).then_inc(O.free(key), 1)
                    else:
                        dve.wait_ge(*O.freed(("y0", b, k - 1)))
                        for t in range(TB):
                            ins = dve.scalar_tensor_tensor(acc[:, b, t, :], y[:, t, :], cw[:, b, t, k - 1:k],
                                                           acc[:, b, t, :], ALU.mult, ALU.add)
                        ins.then_inc(O.free(key), 1)
                    if b == 0 and k == 2:
                        head_blocks()
                    if b == 0 and k == 3:
                        weight_stats()
                    if b == 0 and k == 6:
                        weight_quantise()
                    if b == 1 and k == 2:
                        normalise("L1x", 0)
                dve.wait_ge(*O.freed(("y0", b, E)))
                rows = x[:, b * TB:b * TB + TB, :]
                step(dve.scalar_tensor_tensor(rows, acc[:, b, :, :], G[:, 4:5], rows, ALU.mult, ALU.add))
            normalise("L1x", 1)

            def attention(layer, finish):
                base = T * (layer == "L2x")

                def less_max(n):
                    if n >= 4:
                        dve.wait_ge(*TR.filled(("pT", layer, n - 4, len(TCH) - 1)))
                    for i, (h0, h1) in enumerate(HEADS):
                        key = (layer, n, i)
                        v = S.bank(key)[:, 0:(h1 - h0) * R].rearrange("p (h r) -> p h r", h=h1 - h0)
                        dve.wait_ge(*S.filled(key))
                        step(dve.tensor_reduce(pmax[:, n % 4, h0:h1], v, AX, ALU.max))
                        dve.tensor_tensor(pr4[n % 4][:, h0 * R:h1 * R].rearrange("p (h r) -> p h r", h=h1 - h0), v,
                                          bc(pmax[:, n % 4, h0:h1], R), ALU.subtract).then_inc(S.free(key), 1)

                if layer == "L1x":
                    dve.wait_ge(*S.filled(("h0", B - 1, E, C - 1)))
                less_max(0)
                for n in range(T):
                    if 1 <= n < T - 1:
                        less_max(n + 1)
                    dve.wait_ge(p_exp, base + n + 1)
                    step(dve.tensor_reduce(psums[:, n % 4, 0, :], pr4[n % 4].rearrange("p (h r) -> p h r", h=H),
                                           AX, ALU.add))
                    dve.reciprocal(psums[:, n % 4, 1, :], psums[:, n % 4, 0, :]).then_inc(p_recip, 1)
                    if n == 0:
                        less_max(1)
                finish(0)
                finish(1)

            def finish_l1x(b):
                update(("L1x", b), b, 1)
                normalise("L1f", b)
                dve.wait_ge(*ln_done("L1f", b))
                step(dve.tensor_reduce(hmax[:, 2 * b:2 * b + 1], ln[:, b * TB:b * TB + TB, :].rearrange("p t d -> p (t d)"),
                                       AX, ALU.max, apply_absolute_value=True))

            attention("L1x", finish_l1x)
            dve.tensor_tensor(hmax[:, B * C:B * C + 1], hmax[:, 0:1], hmax[:, 2:3], ALU.max).then_inc(amax_ready, 1)
            dve.wait_ge(amax_all, 1)
            step(dve.tensor_scalar(wsc[:, 3:4], hall[:, 0:1], 1e-6, 1.0 / QP, ALU.max, ALU.mult))
            step(dve.reciprocal(wsc[:, 8:9], wsc[:, 3:4]))
            for b in range(B):
                rows = ln[:, b * TB:b * TB + TB, :]
                q = qtmp[:, b, :, :]
                step(dve.tensor_scalar(q, rows, wsc[:, 8:9], MAGIC, ALU.mult, ALU.add))
                dve.tensor_scalar(xqb[:, b * TB:b * TB + TB, :], q, MAGIC, None, ALU.subtract).then_inc(xq_ready, 1)
            step(dve.tensor_tensor(wsc[:, 2:3], wsc[:, 3:4], wsc[:, 0:1], ALU.mult))
            dve.tensor_scalar(wsc[:, 4:8], fb1[:, :], wsc[:, 2:3], None, ALU.mult).then_inc(s1_ready, 1)
            for b in range(B):
                for c in range(C):
                    dve.wait_ge(*S.freed(("h1", b, c)))
                    ins = dve.tensor_reduce(hmax[:, b * C + c:b * C + c + 1], hT[:, b, c, :], AX, ALU.max,
                                            apply_absolute_value=True)
            step(ins)
            dve.tensor_reduce(hmax[:, B * C + 1:B * C + 2], hmax[:, 0:B * C], AX, ALU.max).then_inc(amax_ready, 1)
            dve.wait_ge(amax_all, 2)
            step(dve.tensor_scalar(wsc[:, 9:10], hall[:, 1:2], 1e-6, 1.0 / QP, ALU.max, ALU.mult))
            step(dve.reciprocal(wsc[:, 10:11], wsc[:, 9:10]))
            for b in range(B):
                v = hT[:, b, :, :]
                step(dve.tensor_scalar(v, v, wsc[:, 10:11], MAGIC, ALU.mult, ALU.add))
                dve.tensor_scalar(hqb[:, :, b * SEQ:b * SEQ + SEQ], v, MAGIC, None, ALU.subtract).then_inc(hq_ready, 1)
            step(dve.tensor_scalar(wsc[:, 11:12], wsc[:, 9:10], wsc[:, 1:2], G[:, 5:6], ALU.mult, ALU.mult))
            for b in range(B):
                key = ("L1f", b)
                q, rows = qtmp[:, b, :, :], x[:, b * TB:b * TB + TB, :]
                dve.wait_ge(*O.filled(key))
                dve.tensor_tensor(q, O.bank(key)[:, :].rearrange("p (t d) -> p t d", t=TB),
                                  b2_1[:, :].unsqueeze(1).to_broadcast([P, TB, D]), ALU.add).then_inc(O.free(key), 1)
                dve.wait_ge(*O.freed(key))
                step(dve.scalar_tensor_tensor(rows, q, wsc[:, 11:12], rows, ALU.mult, ALU.add))
                normalise("L2x", b)

            def finish_l2x(b):
                ts = slice(b * TB, b * TB + TB)
                dve.wait_ge(biased, B + 1 + b + 2)
                update(("o2", b), b, 2)
                normalise("L2f", b)
                dve.wait_ge(*ln_done("L2f", b))
                step(dve.tensor_reduce(tsc[:, 0, ts], ln[:, ts, :], AX, ALU.max, apply_absolute_value=True))
                step(dve.tensor_scalar(tsc[:, 0, ts], tsc[:, 0, ts], 1e-5, 1.0 / QP, ALU.max, ALU.mult))
                step(dve.reciprocal(tsc[:, 1, ts], tsc[:, 0, ts]))
                for t in range(TB):
                    n = b * TB + t
                    ins = dve.tensor_scalar(qtmp[:, b, t, :], ln[:, n, :], tsc[:, 1, n:n + 1], MAGIC, ALU.mult, ALU.add)
                step(ins)
                dve.tensor_scalar(xqb[:, ts, :], qtmp[:, b, :, :], MAGIC, QP, ALU.subtract, ALU.min).then_inc(xq_ready, 1)
                dve.tensor_scalar(tsc[:, 3, ts], tsc[:, 0, ts], wsc[:, 15:16], None, ALU.mult)
                dve.tensor_scalar(tsc[:, 2, ts], tsc[:, 0, ts], wsc[:, 14:15], None, ALU.mult).then_inc(tscale_ready, 1)

            attention("L2x", finish_l2x)
            def down_update(m):
                key = ("L2f", m // TB)
                ins = dve.scalar_tensor_tensor(x[:, m, :], O.bank(key)[:, m % TB * D:(m % TB + 1) * D], tsc[:, 6, m:m + 1],
                                               x[:, m, :], ALU.mult, ALU.add)
                return ins

            for n in range(T + 1):
                if n < T:
                    dve.wait_ge(*S.filled(("up", n)))
                    dve.wait_ge(*S.freed(("gate", n)))
                    g = guf[:, n % 2, :]
                    if n >= 2:
                        dve.wait_ge(gub_ready, n - 1)
                    dve.scalar_tensor_tensor(g, S.bank(("up", n))[:, :], tsc[:, 3, n:n + 1], silu[:, n % 2, :],
                                             ALU.mult, ALU.mult).then_inc(S.free(("up", n)), 1)
                    dve.wait_ge(*S.freed(("up", n)))
                    step(dve.tensor_reduce(tsc[:, 4, n:n + 1], g, AX, ALU.max, apply_absolute_value=True))
                    step(dve.tensor_scalar(tsc[:, 4, n:n + 1], tsc[:, 4, n:n + 1], 1e-5, 1.0 / QP, ALU.max, ALU.mult))
                    dve.reciprocal(tsc[:, 5, n:n + 1], tsc[:, 4, n:n + 1]).then_inc(gscale_ready, 1)
                if n >= 1:
                    m = n - 1
                    if m >= 2:
                        dve.wait_ge(*TR.filled(("guT", m - 2)))
                    dve.wait_ge(gq_ready, m + 1)
                    dve.tensor_scalar(gub[:, m % 2, :], guf[:, m % 2, :], MAGIC, QP, ALU.subtract,
                                      ALU.min).then_inc(gub_ready, 1)
            step(dve.tensor_scalar(tsc[:, 6, :], tsc[:, 4, :], wsc[:, 16:17], G[:, 6:7], ALU.mult, ALU.mult))
            for b in range(B):
                key = ("L2f", b)
                dve.wait_ge(*O.filled(key))
                for m in range(b * TB, b * TB + TB):
                    ins = down_update(m)
                ins.then_inc(O.free(key), 1)
                dve.wait_ge(*O.freed(key))
                normalise("L3x", b)

            for b in range(B):
                softmax_in(("s3", b), b)
            for b in range(B):
                softmax_out(b, B + b + 1)
            for b in range(B):
                update(("L3x", b), b, 3)
                normalise("L3f", b)
            for b in range(B):
                dve.wait_ge(*S.filled(("mean", b)))
                dve.tensor_copy(mean3[:, b:b + 1], S.bank(("mean", b))[:, 0:1]).then_inc(S.free(("mean", b)), 1)
            dve.wait_ge(*loaded("l3f"))
            for b in range(B):
                key = ("pick", b)
                dve.wait_ge(*S.filled(key))
                dve.tensor_tensor(sc3[:, b, :], S.bank(key)[0:1, 0:E], br3[:, :], ALU.add).then_inc(S.free(key), 1)
                dve.wait_ge(*S.freed(key))
                step(dve.max(top3[:, b, :], sc3[:, b, :]))
                step(dve.max_index(top3i[:, b, :], top3[:, b, :], sc3[:, b, :]))
                e = dve.value_load(top3i[0:1, b, 0:1], min_val=0, max_val=E - 1)
                dve.tensor_copy(w1s[:, b, :], ex_flat[:, bass.ds(e * (2 * FF), FF)])
                dve.tensor_copy(w2s[:, b, :], ex_flat[:, bass.ds(e * (2 * FF) + FF, FF)])
                dve.tensor_copy(b2s[:, b, :], b2_flat[:, bass.ds(e * D, D)])
                dve.tensor_copy(b1s[:, b, :], b1_flat[:, bass.ds(e * C, C)]).then_inc(pick_ready, 1)
            for b in range(B):
                rows, key = x[:, b * TB:b * TB + TB, :], ("L3f", b)
                dve.wait_ge(*O.filled(key))
                dve.scalar_tensor_tensor(rows, O.bank(key)[:, :].rearrange("p (t d) -> p t d", t=TB), G[:, 7:8],
                                         rows, ALU.mult, ALU.add).then_inc(x_final, 1)


def layout(i):
    def rows(w, n):
        return w.reshape(n, 128, -1).transpose(1, 0, 2)

    f = {k: np.asarray(v) for k, v in i.items()}
    c = f["ctx_1024"]
    w1 = np.concatenate([f["L0_ffn_w1_shared"][None], f["L0_ffn_w1_routed"]])
    w2 = np.concatenate([f["L0_ffn_w2_shared"][None], f["L0_ffn_w2_routed"]])
    return {
        "x": f["x"], "mask": f["mask_Bx1xSxS2_if1"][:, 0],
        "ctxT": c.transpose(2, 0, 1), "ctx_rows": c.transpose(1, 0, 2),
        "g_xattn": f["g_xattn"], "g_ffn": f["g_ffn"],
        "simw": f["L0_xattn_w_sim"].reshape(3, 128).T, "b_sim": f["L0_xattn_b_sim"].reshape(1, 1),
        "wqv0": rows(f["L0_xattn_W_qv"], 4), "bqv0": f["L0_xattn_b_qv"],
        "w_router": f["L0_ffn_w_router"], "w1_0": w1.transpose(1, 0, 2),
        "w2_0": w2.reshape(9, 4, 128, 128).transpose(2, 0, 1, 3).reshape(128, 9, 512),
        "wqT1": rows(f["L1_xattn_Wq"].T, 8), "wk1": f["L1_xattn_Wk"], "wv1": f["L1_xattn_Wv"],
        "wo1": rows(f["L1_xattn_Wo"], 8),
        "fw1": f["L1_ffn_w1"].T, "fb1": f["L1_ffn_b1"].reshape(4, 128).T, "fw2": rows(f["L1_ffn_w2"].T, 4),
        "b2_1": f["L1_ffn_b2"],
        "w2x": np.stack([f["L2_xattn_W" + k].T for k in "qkvo"], axis=1), "bo2": f["L2_xattn_bo"],
        "fw_gu": np.stack([f["L2_ffn_w_gate"].T, f["L2_ffn_w_up"].T], axis=1), "fw_d": rows(f["L2_ffn_w_down"].T, 4),
        "w3x": np.stack([f["L3_xattn_Wq"], f["L3_xattn_Wk"].T, f["L3_xattn_Wv"].T], axis=1),
        "b3x": np.stack([f["L3_xattn_bq"], f["L3_xattn_bk"]], axis=1), "bv3": f["L3_xattn_bv"][None],
        "wr3": f["L3_ffn_Wr"], "br3": f["L3_ffn_br"][None], "w1_3": f["L3_ffn_W1"].transpose(1, 0, 2),
        "b1_3": f["L3_ffn_b1"].reshape(8, 4, 128).transpose(2, 0, 1),
        "w2_3": f["L3_ffn_W2"].reshape(8, 4, 128, 128).transpose(2, 0, 1, 3).reshape(128, 8, 512),
        "b2_3": f["L3_ffn_b2"].reshape(1, -1),
    }


def kernel(**inputs):
    import concourse.bacc as bacc
    from concourse.bass_utils import run_bass_kernel_spmd

    nc = bacc.Bacc("TRN2", target_bir_lowering=False, num_devices=1)
    arrays, args = {}, {}
    for name, v in layout(inputs).items():
        v = np.ascontiguousarray(v)
        arrays["in_" + name] = v
        args[name] = nc.dram_tensor("in_" + name, v.shape, mybir.dt.from_np(v.dtype), kind="ExternalInput").ap()
    out = nc.dram_tensor("out_x", (B, SEQ, D), F32, kind="ExternalOutput").ap()
    program(nc, args, out)
    r = run_bass_kernel_spmd(nc, [arrays], core_ids=[0])
    return r.results[0]["out_x"]
```
